# Optimizing a Trainium2 kernel written in Bass

```python
import numpy as np
import jax
import jax.numpy as jnp

def _softmax(x, axis=-1):
    return jax.nn.softmax(x, axis=axis)

def _gelu(x):
    return jax.nn.gelu(x, approximate=True)

def _silu(x):
    return jax.nn.silu(x)

def _sigmoid(x):
    return jax.nn.sigmoid(x)

def _layernorm(x, axis=-1, eps=1e-05):
    m = jnp.mean(x, axis=axis, keepdims=True)
    v = jnp.var(x, axis=axis, keepdims=True)
    return (x - m) / jnp.sqrt(v + eps)

def _scatter_add(tgt, idx, src, axis=0):
    return tgt.at[idx].add(src)

def _segment_sum(src, seg, n):
    return jax.ops.segment_sum(src, seg, n)
kernel_name = 'mk_perceiver_d2_seqx_r4_a83f61'

def setup_inputs(seed: int=0):
    np.random.seed(seed)
    _w = jnp.asarray

    def _rec_inputs():
        import jax
        import jax.numpy as jnp
        _rk = jax.random.key(seed)
        x = -0.0002928 + 1 * jax.random.normal(jax.random.fold_in(_rk, 1), (16, 64, 256), jnp.float32)
        _lenS = 64 - jax.random.randint(jax.random.fold_in(_rk, 7), (16,), 0, max(1, 64 // 4) + 1, jnp.int32)
        _lenS2 = 1601 - jax.random.randint(jax.random.fold_in(_rk, 8), (16,), 0, max(1, 1601 // 4) + 1, jnp.int32)
        _ctx_1024P = jax.random.normal(jax.random.fold_in(_rk, 11), (16, 16, 256), jnp.float32)
        _ctx_1024c = jax.random.dirichlet(jax.random.fold_in(_rk, 511), 0.3 * jnp.ones((16,), jnp.float32), (16, 1601))
        _ctx_1024t = jnp.einsum('bsk,bkd->bsd', _ctx_1024c, _ctx_1024P)
        _ctx_1024t = _ctx_1024t * jax.lax.rsqrt(jnp.mean(jnp.square(_ctx_1024t)) + 1e-12) * 0.953939
        ctx_1024 = -1.39393e-06 + 0.999914 * (_ctx_1024t + 0.3 * jax.random.normal(jax.random.fold_in(_rk, 611), (16, 1601, 256), jnp.float32))
        _validS = jnp.arange(64)[None, :] < _lenS[:, None]
        _validS2 = jnp.arange(1601)[None, :] < _lenS2[:, None]
        _causal = jnp.tril(jnp.ones((64, 64), dtype=bool))
        mask_B_ik0 = jnp.where(jnp.ones((16,), dtype=bool), 68, 1563).astype(jnp.int32)
        mask_Bx1xSxS2_fk0 = jnp.where(jnp.broadcast_to(_validS2[:, None, None, :], (16, 1, 64, 1601)), 0.0, 1.0).astype(jnp.float32)
        return (x, ctx_1024, mask_B_ik0, mask_Bx1xSxS2_fk0)
    x, ctx_1024, mask_B_ik0, mask_Bx1xSxS2_fk0 = _rec_inputs()

    def _L0_xattn_setup():
        import jax, jax.numpy as jnp
        import numpy as np
        B, S, D, H = (2, 512, 256, 16)
        DH = D // H

        def _split_heads(x):
            b, s, _ = x.shape
            return x.reshape(b, s, H, DH).transpose(0, 2, 1, 3)
        key = jax.random.key(seed)
        k = jax.random.split(key, 8)
        scale = 0.02
        return {'queries': jax.random.normal(k[0], (B, S, D), dtype=jnp.float32), 'keys': jax.random.normal(k[1], (B, S, D), dtype=jnp.float32), 'values': jax.random.normal(k[2], (B, S, D), dtype=jnp.float32), 'valid_length': jax.random.randint(k[3], (B,), 0, S, dtype=jnp.int64), 'Wq': jax.random.normal(k[4], (D, D), dtype=jnp.float32) * scale, 'Wk': jax.random.normal(k[5], (D, D), dtype=jnp.float32) * scale, 'Wv': jax.random.normal(k[6], (D, D), dtype=jnp.float32) * scale, 'Wo': jax.random.normal(k[7], (D, D), dtype=jnp.float32) * scale}
    _L0_xattn_all = _L0_xattn_setup()
    _L0_xattn_in = {k: v for k, v in _L0_xattn_all.items() if k in ('Wq', 'Wk', 'Wv', 'Wo')}
    del _L0_xattn_all

    def _L0_attn_setup():
        import jax, jax.numpy as jnp
        import numpy as np
        B, T, C = (8, 512, 256)
        EPS_LN = 1e-05
        EPS_WKV = 1e-08

        def layer_norm(x, g, b):
            mu = jnp.mean(x, axis=-1, keepdims=True)
            var = jnp.var(x, axis=-1, keepdims=True)
            return (x - mu) * jax.lax.rsqrt(var + EPS_LN) * g + b

        def time_shift(x, ratio):
            x_prev = jnp.pad(x[:, :-1, :], ((0, 0), (1, 0), (0, 0)))
            return x * ratio + x_prev * (1.0 - ratio)

        def wkv(w, u, k, v):
            kT = jnp.swapaxes(k, 0, 1)
            vT = jnp.swapaxes(v, 0, 1)
            aa0 = jnp.zeros((k.shape[0], k.shape[2]), k.dtype)
            ninf = jnp.full_like(aa0, -jnp.inf)

            def step(carry, kv):
                aa, bb, pp = carry
                kk, vv = kv
                ww = u + kk
                p = jnp.maximum(pp, ww)
                e1 = jnp.exp(pp - p)
                e2 = jnp.exp(ww - p)
                out = (e1 * aa + e2 * vv) / (e1 + e2 + EPS_WKV)
                bb_new = w + pp
                p2 = jnp.maximum(pp, kk)
                e1b = jnp.exp(pp - p2)
                e2b = jnp.exp(kk - p2)
                aa_new = e1b * aa + e2b * vv
                pp_new = p2 + jnp.log(e1b + e2b + EPS_WKV)
                return ((aa_new, bb_new, pp_new), out)
            (aa, bb, pp), outT = jax.lax.scan(step, (aa0, ninf, ninf), (kT, vT))
            output = jnp.swapaxes(outT, 0, 1)
            final_state = jnp.stack([aa, bb, pp], axis=2)
            return (output, final_state)

        def _reference_tuple_inner(x, time_decay, time_first, Wk_t, Wv_t, Wr_t, Wk_c, Wv_c, Wr_c, ln1_g, ln1_b, ln2_g, ln2_b, mix_k, mix_v, mix_r, cmix_k, cmix_r):
            h = layer_norm(x, ln1_g, ln1_b)
            k = time_shift(h, mix_k) @ Wk_t.T
            v = time_shift(h, mix_v) @ Wv_t.T
            r = jax.nn.sigmoid(time_shift(h, mix_r) @ Wr_t.T)
            w = -jnp.exp(time_decay)
            wkv_out, new_state = wkv(w, time_first, k, v)
            x = x + r * wkv_out
            h2 = layer_norm(x, ln2_g, ln2_b)
            kc = time_shift(h2, cmix_k) @ Wk_c.T
            rc = jax.nn.sigmoid(time_shift(h2, cmix_r) @ Wr_c.T)
            vv = jnp.square(jax.nn.relu(kc)) @ Wv_c.T
            x = x + rc * vv
            return (x, new_state)
        key = jax.random.key(seed)
        ks = jax.random.split(key, 16)
        s = 1.0 / np.sqrt(C)
        inp = {'x': jax.random.normal(ks[0], (B, T, C), jnp.float32), 'time_decay': jax.random.normal(ks[1], (C,), jnp.float32), 'time_first': jax.random.normal(ks[2], (C,), jnp.float32), 'Wk_t': jax.random.normal(ks[3], (C, C), jnp.float32) * s, 'Wv_t': jax.random.normal(ks[4], (C, C), jnp.float32) * s, 'Wr_t': jax.random.normal(ks[5], (C, C), jnp.float32) * s, 'Wk_c': jax.random.normal(ks[6], (4 * C, C), jnp.float32) * s, 'Wv_c': jax.random.normal(ks[7], (C, 4 * C), jnp.float32) * (0.5 * s), 'Wr_c': jax.random.normal(ks[8], (C, C), jnp.float32) * s, 'ln1_g': jnp.ones((C,), jnp.float32), 'ln1_b': jnp.zeros((C,), jnp.float32), 'ln2_g': jnp.ones((C,), jnp.float32), 'ln2_b': jnp.zeros((C,), jnp.float32), 'mix_k': jnp.ones((C,), jnp.float32), 'mix_v': jnp.ones((C,), jnp.float32), 'mix_r': jnp.ones((C,), jnp.float32), 'cmix_k': jnp.ones((C,), jnp.float32), 'cmix_r': jnp.ones((C,), jnp.float32)}
        return inp
    _L0_attn_all = _L0_attn_setup()
    _L0_attn_in = {k: v for k, v in _L0_attn_all.items() if k in ('time_decay', 'time_first', 'Wk_t', 'Wv_t', 'Wr_t', 'Wk_c', 'Wv_c', 'Wr_c', 'ln1_g', 'ln1_b', 'ln2_g', 'ln2_b', 'mix_k', 'mix_v', 'mix_r', 'cmix_k', 'cmix_r')}
    del _L0_attn_all

    def _L0_ffn_setup():
        import jax, jax.numpy as jnp
        import numpy as np
        B, S, D, E, F = (2, 512, 256, 8, 1024)
        key = jax.random.key(seed)
        ks = jax.random.split(key, 4)
        return {'hidden_states': jax.random.normal(ks[0], (B, S, D), dtype=jnp.float32), 'Wr': jax.random.normal(ks[1], (D, E), dtype=jnp.float32) * (1.0 / np.sqrt(D)), 'W1': jax.random.normal(ks[2], (E, D, F), dtype=jnp.float32) * (1.0 / np.sqrt(D)), 'b1': jnp.zeros((E, F), dtype=jnp.float32), 'W2': jax.random.normal(ks[3], (E, F, D), dtype=jnp.float32) * (1.0 / np.sqrt(F)), 'b2': jnp.zeros((E, D), dtype=jnp.float32)}
    _L0_ffn_all = _L0_ffn_setup()
    _L0_ffn_in = {k: v for k, v in _L0_ffn_all.items() if k in ('Wr', 'W1', 'b1', 'W2', 'b2')}
    del _L0_ffn_all

    def _L1_xattn_setup():
        import jax, jax.numpy as jnp
        import numpy as np
        D_MODEL = 256
        N_HEADS = 16
        DEPTH = D_MODEL // N_HEADS
        B, S = (2, 512)

        def _split_heads(x):
            b, s, _ = x.shape
            return x.reshape(b, s, N_HEADS, DEPTH).transpose(0, 2, 1, 3)
        key = jax.random.key(seed)
        ks = jax.random.split(key, 13)
        scale = 1.0 / np.sqrt(D_MODEL)
        inp = {'query': jax.random.normal(ks[0], (B, S, D_MODEL), jnp.float32), 'key': jax.random.normal(ks[1], (B, S, D_MODEL), jnp.float32), 'value': jax.random.normal(ks[2], (B, S, D_MODEL), jnp.float32), 'mask': (jax.random.uniform(ks[3], (B, 1, S, S)) < 0.1).astype(jnp.float32), 'Wq': jax.random.normal(ks[4], (D_MODEL, D_MODEL), jnp.float32) * scale, 'bq': jnp.zeros((D_MODEL,), jnp.float32), 'Wk': jax.random.normal(ks[5], (D_MODEL, D_MODEL), jnp.float32) * scale, 'bk': jnp.zeros((D_MODEL,), jnp.float32), 'Wv': jax.random.normal(ks[6], (D_MODEL, D_MODEL), jnp.float32) * scale, 'bv': jnp.zeros((D_MODEL,), jnp.float32), 'Wo': jax.random.normal(ks[7], (D_MODEL, D_MODEL), jnp.float32) * scale, 'bo': jnp.zeros((D_MODEL,), jnp.float32)}
        return inp
    _L1_xattn_all = _L1_xattn_setup()
    _L1_xattn_in = {k: v for k, v in _L1_xattn_all.items() if k in ('Wq', 'bq', 'Wk', 'bk', 'Wv', 'bv', 'Wo', 'bo')}
    del _L1_xattn_all

    def _L1_attn_setup():
        import math
        import jax, jax.numpy as jnp
        import numpy as np
        E = 256
        H = 16
        KVH = 8
        N_REP = H // KVH
        HD = E // H // 2
        DEPTH = 12
        LAMBDA_INIT = 0.8 - 0.6 * math.exp(-0.3 * DEPTH)
        EPS = 1e-06
        ROPE_BASE = 10000.0

        def rope_tables(T):
            inv_freq = 1.0 / ROPE_BASE ** (np.arange(0, HD, 2, dtype=np.float32) / HD)
            t = np.arange(T, dtype=np.float32)
            freqs = np.outer(t, inv_freq)
            return (jnp.asarray(np.cos(freqs)), jnp.asarray(np.sin(freqs)))

        def apply_rope(x, cos, sin):
            d = x.shape[-1] // 2
            c = cos[None, :, None, :]
            s = sin[None, :, None, :]
            x1, x2 = (x[..., :d], x[..., d:])
            return jnp.concatenate([x1 * c + x2 * s, -x1 * s + x2 * c], axis=-1)

        def causal_attn(q, k, v, scale):
            T = q.shape[1]
            mask = jnp.tril(jnp.ones((T, T), dtype=bool))
            s = jnp.einsum('bthd,bshd->bhts', q, k) * scale
            s = jnp.where(mask[None, None], s, jnp.finfo(s.dtype).min)
            p = jax.nn.softmax(s, axis=-1)
            return jnp.einsum('bhts,bshd->bthd', p, v)
        key = jax.random.key(seed)
        ks = jax.random.split(key, 10)
        s = 0.02
        return {'x': jax.random.normal(ks[0], (4, 256, E), jnp.float32), 'Wq': jax.random.normal(ks[1], (E, E), jnp.float32) * s, 'Wk': jax.random.normal(ks[2], (E, E // N_REP), jnp.float32) * s, 'Wv': jax.random.normal(ks[3], (E, E // N_REP), jnp.float32) * s, 'Wo': jax.random.normal(ks[4], (E, E), jnp.float32) * s, 'lambda_q1': jax.random.normal(ks[5], (HD,), jnp.float32) * 0.1, 'lambda_k1': jax.random.normal(ks[6], (HD,), jnp.float32) * 0.1, 'lambda_q2': jax.random.normal(ks[7], (HD,), jnp.float32) * 0.1, 'lambda_k2': jax.random.normal(ks[8], (HD,), jnp.float32) * 0.1, 'rms_w': jnp.ones((2 * HD,), jnp.float32)}
    _L1_attn_all = _L1_attn_setup()
    _L1_attn_in = {k: v for k, v in _L1_attn_all.items() if k in ('Wq', 'Wk', 'Wv', 'Wo', 'lambda_q1', 'lambda_k1', 'lambda_q2', 'lambda_k2', 'rms_w')}
    del _L1_attn_all

    def _L1_ffn_setup():
        import jax, jax.numpy as jnp
        import numpy as np
        CAPACITY_RATIO = 0.75
        key = jax.random.key(seed)
        k1, k2, k3 = jax.random.split(key, 3)
        B, L, D = (4, 2048, 256)
        x = jax.random.normal(k1, (B, L, D), dtype=jnp.float32)
        w_router = jax.random.normal(k2, (D,), dtype=jnp.float32) * 0.02
        w_block = jax.random.normal(k3, (D, D), dtype=jnp.float32) * 0.02
        return {'x': x, 'w_router': w_router, 'w_block': w_block}
    _L1_ffn_all = _L1_ffn_setup()
    _L1_ffn_in = {k: v for k, v in _L1_ffn_all.items() if k in ('w_router', 'w_block')}
    del _L1_ffn_all
    return {'x': x, 'ctx_1024': ctx_1024, 'mask_B_ik0': mask_B_ik0, 'mask_Bx1xSxS2_fk0': mask_Bx1xSxS2_fk0, 'L0_xattn_Wq': _L0_xattn_in['Wq'], 'L0_xattn_Wk': _L0_xattn_in['Wk'], 'L0_xattn_Wv': _L0_xattn_in['Wv'], 'L0_xattn_Wo': _L0_xattn_in['Wo'], 'L0_attn_time_decay': _L0_attn_in['time_decay'], 'L0_attn_time_first': _L0_attn_in['time_first'], 'L0_attn_Wk_t': _L0_attn_in['Wk_t'], 'L0_attn_Wv_t': _L0_attn_in['Wv_t'], 'L0_attn_Wr_t': _L0_attn_in['Wr_t'], 'L0_attn_Wk_c': _L0_attn_in['Wk_c'], 'L0_attn_Wv_c': _L0_attn_in['Wv_c'], 'L0_attn_Wr_c': _L0_attn_in['Wr_c'], 'L0_attn_ln1_g': _L0_attn_in['ln1_g'], 'L0_attn_ln1_b': _L0_attn_in['ln1_b'], 'L0_attn_ln2_g': _L0_attn_in['ln2_g'], 'L0_attn_ln2_b': _L0_attn_in['ln2_b'], 'L0_attn_mix_k': _L0_attn_in['mix_k'], 'L0_attn_mix_v': _L0_attn_in['mix_v'], 'L0_attn_mix_r': _L0_attn_in['mix_r'], 'L0_attn_cmix_k': _L0_attn_in['cmix_k'], 'L0_attn_cmix_r': _L0_attn_in['cmix_r'], 'L0_ffn_Wr': _L0_ffn_in['Wr'], 'L0_ffn_W1': _L0_ffn_in['W1'], 'L0_ffn_b1': _L0_ffn_in['b1'], 'L0_ffn_W2': _L0_ffn_in['W2'], 'L0_ffn_b2': _L0_ffn_in['b2'], 'L1_xattn_Wq': _L1_xattn_in['Wq'], 'L1_xattn_bq': _L1_xattn_in['bq'], 'L1_xattn_Wk': _L1_xattn_in['Wk'], 'L1_xattn_bk': _L1_xattn_in['bk'], 'L1_xattn_Wv': _L1_xattn_in['Wv'], 'L1_xattn_bv': _L1_xattn_in['bv'], 'L1_xattn_Wo': _L1_xattn_in['Wo'], 'L1_xattn_bo': _L1_xattn_in['bo'], 'L1_attn_Wq': _L1_attn_in['Wq'], 'L1_attn_Wk': _L1_attn_in['Wk'], 'L1_attn_Wv': _L1_attn_in['Wv'], 'L1_attn_Wo': _L1_attn_in['Wo'], 'L1_attn_lambda_q1': _L1_attn_in['lambda_q1'], 'L1_attn_lambda_k1': _L1_attn_in['lambda_k1'], 'L1_attn_lambda_q2': _L1_attn_in['lambda_q2'], 'L1_attn_lambda_k2': _L1_attn_in['lambda_k2'], 'L1_attn_rms_w': _L1_attn_in['rms_w'], 'L1_ffn_w_router': _L1_ffn_in['w_router'], 'L1_ffn_w_block': _L1_ffn_in['w_block']}

def reference(x, ctx_1024, mask_B_ik0, mask_Bx1xSxS2_fk0, L0_xattn_Wq, L0_xattn_Wk, L0_xattn_Wv, L0_xattn_Wo, L0_attn_time_decay, L0_attn_time_first, L0_attn_Wk_t, L0_attn_Wv_t, L0_attn_Wr_t, L0_attn_Wk_c, L0_attn_Wv_c, L0_attn_Wr_c, L0_attn_ln1_g, L0_attn_ln1_b, L0_attn_ln2_g, L0_attn_ln2_b, L0_attn_mix_k, L0_attn_mix_v, L0_attn_mix_r, L0_attn_cmix_k, L0_attn_cmix_r, L0_ffn_Wr, L0_ffn_W1, L0_ffn_b1, L0_ffn_W2, L0_ffn_b2, L1_xattn_Wq, L1_xattn_bq, L1_xattn_Wk, L1_xattn_bk, L1_xattn_Wv, L1_xattn_bv, L1_xattn_Wo, L1_xattn_bo, L1_attn_Wq, L1_attn_Wk, L1_attn_Wv, L1_attn_Wo, L1_attn_lambda_q1, L1_attn_lambda_k1, L1_attn_lambda_q2, L1_attn_lambda_k2, L1_attn_rms_w, L1_ffn_w_router, L1_ffn_w_block):
    import jax
    import jax.numpy as jnp

    def _L0_xattn_ref(queries, keys, values, valid_length, Wq, Wk, Wv, Wo):
        import jax, jax.numpy as jnp
        import numpy as np
        B, S, D, H = (2, 512, 256, 16)
        DH = D // H

        def _split_heads(x):
            b, s, _ = x.shape
            return x.reshape(b, s, H, DH).transpose(0, 2, 1, 3)
        q = _split_heads(queries @ Wq)
        k = _split_heads(keys @ Wk)
        v = _split_heads(values @ Wv)
        scores = jnp.einsum('bhqd,bhkd->bhqk', q, k)
        attn = jax.nn.softmax(scores, axis=-1)
        out = jnp.einsum('bhqk,bhkd->bhqd', attn, v)
        out = out.transpose(0, 2, 1, 3).reshape(queries.shape[0], queries.shape[1], D)
        return out @ Wo

    def _L0_attn_ref(x, time_decay, time_first, Wk_t, Wv_t, Wr_t, Wk_c, Wv_c, Wr_c, ln1_g, ln1_b, ln2_g, ln2_b, mix_k, mix_v, mix_r, cmix_k, cmix_r):
        import jax, jax.numpy as jnp
        import numpy as np
        B, T, C = (8, 512, 256)
        EPS_LN = 1e-05
        EPS_WKV = 1e-08

        def layer_norm(x, g, b):
            mu = jnp.mean(x, axis=-1, keepdims=True)
            var = jnp.var(x, axis=-1, keepdims=True)
            return (x - mu) * jax.lax.rsqrt(var + EPS_LN) * g + b

        def time_shift(x, ratio):
            x_prev = jnp.pad(x[:, :-1, :], ((0, 0), (1, 0), (0, 0)))
            return x * ratio + x_prev * (1.0 - ratio)

        def wkv(w, u, k, v):
            kT = jnp.swapaxes(k, 0, 1)
            vT = jnp.swapaxes(v, 0, 1)
            aa0 = jnp.zeros((k.shape[0], k.shape[2]), k.dtype)
            ninf = jnp.full_like(aa0, -jnp.inf)

            def step(carry, kv):
                aa, bb, pp = carry
                kk, vv = kv
                ww = u + kk
                p = jnp.maximum(pp, ww)
                e1 = jnp.exp(pp - p)
                e2 = jnp.exp(ww - p)
                out = (e1 * aa + e2 * vv) / (e1 + e2 + EPS_WKV)
                bb_new = w + pp
                p2 = jnp.maximum(pp, kk)
                e1b = jnp.exp(pp - p2)
                e2b = jnp.exp(kk - p2)
                aa_new = e1b * aa + e2b * vv
                pp_new = p2 + jnp.log(e1b + e2b + EPS_WKV)
                return ((aa_new, bb_new, pp_new), out)
            (aa, bb, pp), outT = jax.lax.scan(step, (aa0, ninf, ninf), (kT, vT))
            output = jnp.swapaxes(outT, 0, 1)
            final_state = jnp.stack([aa, bb, pp], axis=2)
            return (output, final_state)

        def _reference_tuple_inner(x, time_decay, time_first, Wk_t, Wv_t, Wr_t, Wk_c, Wv_c, Wr_c, ln1_g, ln1_b, ln2_g, ln2_b, mix_k, mix_v, mix_r, cmix_k, cmix_r):
            h = layer_norm(x, ln1_g, ln1_b)
            k = time_shift(h, mix_k) @ Wk_t.T
            v = time_shift(h, mix_v) @ Wv_t.T
            r = jax.nn.sigmoid(time_shift(h, mix_r) @ Wr_t.T)
            w = -jnp.exp(time_decay)
            wkv_out, new_state = wkv(w, time_first, k, v)
            x = x + r * wkv_out
            h2 = layer_norm(x, ln2_g, ln2_b)
            kc = time_shift(h2, cmix_k) @ Wk_c.T
            rc = jax.nn.sigmoid(time_shift(h2, cmix_r) @ Wr_c.T)
            vv = jnp.square(jax.nn.relu(kc)) @ Wv_c.T
            x = x + rc * vv
            return (x, new_state)
        return _reference_tuple_inner(x, time_decay, time_first, Wk_t, Wv_t, Wr_t, Wk_c, Wv_c, Wr_c, ln1_g, ln1_b, ln2_g, ln2_b, mix_k, mix_v, mix_r, cmix_k, cmix_r)[0]

    def _L0_ffn_ref(hidden_states, Wr, W1, b1, W2, b2):
        import jax, jax.numpy as jnp
        import numpy as np
        B, S, D, E, F = (2, 512, 256, 8, 1024)
        b, s, d = hidden_states.shape
        e = Wr.shape[1]
        x = hidden_states.reshape(b * s, d)
        router_logits = x @ Wr
        router_probs = jax.nn.softmax(router_logits, axis=-1)
        expert_idx = jnp.argmax(router_probs, axis=-1)
        p_max = jnp.max(router_probs, axis=-1, keepdims=True)

        def expert_mlp(w1, bb1, w2, bb2):
            h = jax.nn.gelu(x @ w1 + bb1, approximate=False)
            return h @ w2 + bb2
        outs = jax.vmap(expert_mlp)(W1, b1, W2, b2)
        onehot = jax.nn.one_hot(expert_idx, e, dtype=x.dtype)
        next_states = jnp.einsum('te,etd->td', onehot, outs)
        out = p_max * next_states
        return out.reshape(b, s, d)

    def _L1_xattn_ref(query, key, value, mask, Wq, bq, Wk, bk, Wv, bv, Wo, bo):
        import jax, jax.numpy as jnp
        import numpy as np
        D_MODEL = 256
        N_HEADS = 16
        DEPTH = D_MODEL // N_HEADS
        B, S = (2, 512)

        def _split_heads(x):
            b, s, _ = x.shape
            return x.reshape(b, s, N_HEADS, DEPTH).transpose(0, 2, 1, 3)
        q = _split_heads(query @ Wq.T + bq)
        k = _split_heads(key @ Wk.T + bk)
        v = _split_heads(value @ Wv.T + bv)
        scores = jnp.einsum('bhqd,bhkd->bhqk', q, k) / jnp.sqrt(jnp.float32(DEPTH))
        scores = scores + mask * jnp.float32(-1000000000.0)
        weights = jax.nn.softmax(scores, axis=-1)
        ctx = jnp.einsum('bhqk,bhkd->bhqd', weights, v)
        ctx = ctx.transpose(0, 2, 1, 3).reshape(query.shape[0], -1, D_MODEL)
        return ctx @ Wo.T + bo

    def _L1_attn_ref(x, Wq, Wk, Wv, Wo, lambda_q1, lambda_k1, lambda_q2, lambda_k2, rms_w):
        import math
        import jax, jax.numpy as jnp
        import numpy as np
        E = 256
        H = 16
        KVH = 8
        N_REP = H // KVH
        HD = E // H // 2
        DEPTH = 12
        LAMBDA_INIT = 0.8 - 0.6 * math.exp(-0.3 * DEPTH)
        EPS = 1e-06
        ROPE_BASE = 10000.0

        def rope_tables(T):
            inv_freq = 1.0 / ROPE_BASE ** (np.arange(0, HD, 2, dtype=np.float32) / HD)
            t = np.arange(T, dtype=np.float32)
            freqs = np.outer(t, inv_freq)
            return (jnp.asarray(np.cos(freqs)), jnp.asarray(np.sin(freqs)))

        def apply_rope(x, cos, sin):
            d = x.shape[-1] // 2
            c = cos[None, :, None, :]
            s = sin[None, :, None, :]
            x1, x2 = (x[..., :d], x[..., d:])
            return jnp.concatenate([x1 * c + x2 * s, -x1 * s + x2 * c], axis=-1)

        def causal_attn(q, k, v, scale):
            T = q.shape[1]
            mask = jnp.tril(jnp.ones((T, T), dtype=bool))
            s = jnp.einsum('bthd,bshd->bhts', q, k) * scale
            s = jnp.where(mask[None, None], s, jnp.finfo(s.dtype).min)
            p = jax.nn.softmax(s, axis=-1)
            return jnp.einsum('bhts,bshd->bthd', p, v)
        B, T, _ = x.shape
        q = (x @ Wq).reshape(B, T, 2 * H, HD)
        k = (x @ Wk).reshape(B, T, 2 * KVH, HD)
        v = (x @ Wv).reshape(B, T, KVH, 2, HD)
        cos, sin = rope_tables(T)
        q = apply_rope(q, cos, sin)
        k = apply_rope(k, cos, sin)
        q = q.reshape(B, T, H, 2, HD)
        k = k.reshape(B, T, KVH, 2, HD)
        q1, q2 = (q[:, :, :, 0], q[:, :, :, 1])
        k1, k2 = (k[:, :, :, 0], k[:, :, :, 1])
        vcat = v.reshape(B, T, KVH, 2 * HD)
        k1 = jnp.repeat(k1, N_REP, axis=2)
        k2 = jnp.repeat(k2, N_REP, axis=2)
        vcat = jnp.repeat(vcat, N_REP, axis=2)
        scale = HD ** (-0.5)
        attn1 = causal_attn(q1, k1, vcat, scale)
        attn2 = causal_attn(q2, k2, vcat, scale)
        lambda_1 = jnp.exp(jnp.sum(lambda_q1 * lambda_k1))
        lambda_2 = jnp.exp(jnp.sum(lambda_q2 * lambda_k2))
        lambda_full = lambda_1 - lambda_2 + LAMBDA_INIT
        attn = attn1 - lambda_full * attn2
        rms = jnp.sqrt(jnp.mean(attn * attn, axis=-1, keepdims=True) + EPS)
        attn = attn / rms * rms_w
        attn = attn * (1.0 - LAMBDA_INIT)
        attn = attn.reshape(B, T, H * 2 * HD)
        return attn @ Wo

    def _L1_ffn_ref(x, w_router, w_block):
        import jax, jax.numpy as jnp
        import numpy as np
        CAPACITY_RATIO = 0.75
        B, L, D = x.shape
        k = max(1, int(L * CAPACITY_RATIO))
        scores = jnp.einsum('bld,d->bl', x, w_router)
        _, top_idx = jax.lax.top_k(scores, k)
        selected = jnp.take_along_axis(x, top_idx[:, :, None], axis=1)
        processed = jax.nn.gelu(jnp.einsum('bkd,de->bke', selected, w_block))
        batch_idx = jnp.arange(B)[:, None]
        out = x.at[batch_idx, top_idx].set(processed)
        return out
    x = x + _L0_xattn_ref(_layernorm(x, axis=-1), ctx_1024, ctx_1024, mask_B_ik0, L0_xattn_Wq, L0_xattn_Wk, L0_xattn_Wv, L0_xattn_Wo)
    x = x + _L0_attn_ref(_layernorm(x, axis=-1), L0_attn_time_decay, L0_attn_time_first, L0_attn_Wk_t, L0_attn_Wv_t, L0_attn_Wr_t, L0_attn_Wk_c, L0_attn_Wv_c, L0_attn_Wr_c, L0_attn_ln1_g, L0_attn_ln1_b, L0_attn_ln2_g, L0_attn_ln2_b, L0_attn_mix_k, L0_attn_mix_v, L0_attn_mix_r, L0_attn_cmix_k, L0_attn_cmix_r)
    x = x + _L0_ffn_ref(_layernorm(x, axis=-1), L0_ffn_Wr, L0_ffn_W1, L0_ffn_b1, L0_ffn_W2, L0_ffn_b2)
    x = x + _L1_xattn_ref(_layernorm(x, axis=-1), ctx_1024, ctx_1024, mask_Bx1xSxS2_fk0, L1_xattn_Wq, L1_xattn_bq, L1_xattn_Wk, L1_xattn_bk, L1_xattn_Wv, L1_xattn_bv, L1_xattn_Wo, L1_xattn_bo)
    x = x + _L1_attn_ref(_layernorm(x, axis=-1), L1_attn_Wq, L1_attn_Wk, L1_attn_Wv, L1_attn_Wo, L1_attn_lambda_q1, L1_attn_lambda_k1, L1_attn_lambda_q2, L1_attn_lambda_k2, L1_attn_rms_w)
    x = x + _L1_ffn_ref(_layernorm(x, axis=-1), L1_ffn_w_router, L1_ffn_w_block)
    return x

_drawn_inputs = setup_inputs


def setup_inputs(seed=0):
    import zlib

    import numpy as np

    out = dict(_drawn_inputs(seed))
    spreads = {'L0_attn_ln1_g': (1.0, 0.2),
     'L0_attn_ln1_b': (0.0, 0.1),
     'L0_attn_ln2_g': (1.0, 0.2),
     'L0_attn_ln2_b': (0.0, 0.1),
     'L0_attn_mix_k': (1.0, 0.2),
     'L0_attn_mix_v': (1.0, 0.2),
     'L0_attn_mix_r': (1.0, 0.2),
     'L0_attn_cmix_k': (1.0, 0.2),
     'L0_attn_cmix_r': (1.0, 0.2),
     'L0_ffn_b1': (0.0, 0.305),
     'L0_ffn_b2': (0.0, 0.279),
     'L1_xattn_bq': (0.0, 0.8),
     'L1_xattn_bk': (0.0, 2.0),
     'L1_xattn_bv': (0.0, 0.1),
     'L1_xattn_bo': (0.0, 0.1),
     'L1_attn_rms_w': (1.0, 0.6)}
    factors = {'L1_attn_lambda_q1': 15.401,
     'L1_attn_lambda_k1': 4.72,
     'L1_attn_lambda_q2': 82.968,
     'L1_attn_lambda_k2': 15.785,
     'L0_xattn_Wq': 2.742,
     'L1_attn_Wq': 3.282,
     'L1_attn_Wk': 4.525}
    for name, (base, spread) in spreads.items():
        noise = np.random.default_rng([zlib.crc32(name.encode()), seed]).standard_normal(out[name].shape)
        drawn = base * np.exp(spread * noise) if base else spread * noise
        out[name] = jnp.asarray(drawn.astype(out[name].dtype))
    for name, factor in factors.items():
        out[name] = (out[name] * factor).astype(out[name].dtype)
    return out
```

```python
from contextlib import ExitStack

import numpy as np

import concourse.bass as bass
from concourse import mybir

F32 = mybir.dt.float32
F32R = mybir.dt.float32r
ACT = mybir.ActivationFunctionType
ALU = mybir.AluOpType
AX = mybir.AxisListType

P = 128
NB, T, D, KEYS = 16, 64, 256, 1601
TOK = NB * T
NT = TOK // P
HALVES = D // P
BANK = 512
PAIRS = 8
PW = 32
KT = (KEYS + P - 1) // P
KPAD = KEYS + 1
NEG = -1.0e30
EPS_LN = 1e-5

CONST = {}


def shape_constants():
    r = np.arange(P)
    parts = []

    def put(name, a):
        a = np.asarray(a, np.float32)
        full = np.zeros((P, a.shape[1]), np.float32)
        full[:a.shape[0]] = a
        CONST[name] = (sum(x.shape[1] for x in parts), a.shape[1])
        parts.append(full)

    put("ident", np.eye(P))
    put("qmask", [[float(x // 32 == pl and x % 32 // 16 == hh) for pl in range(4) for hh in range(2)] for x in r])
    put("head_of_pair", [[float(x % 32 // 16 == hh) for hh in range(2)] for x in r])
    put("pair_to_channels", [[float(k == 4 * h + c // 32) for h in range(2) for c in range(P)] for k in range(PAIRS)])
    put("same_query", [[float(x % T == c % T) for c in range(P)] for x in r])
    put("same_sequence", [[float(x // T == c // T) for c in range(P)] for x in r])
    put("own_column", [[float(x % T == c) for c in range(T)] for x in r])
    put("earlier_column", [[float(c < x % T) for c in range(T)] for x in r])
    put("causal", [[0.0 if c <= x % T else NEG for c in range(T)] for x in r])
    put("restart", [[NEG if c == 0 else 0.0 for c in range(T)] for x in r])
    put("row_half_of_head", [[float(c // 16 % 2 == x // T) for c in range(P)] for x in r])
    put("unit_rows", [[float(x // 8 == u) for u in range(16)] for x in r])
    put("expert_order", [[float(8 - e) for e in range(8)] for x in r])
    inv = 1.0 / 10000.0 ** (np.arange(0, 8, 2, dtype=np.float32) / 8)
    freqs = np.outer(np.arange(T, dtype=np.float32), inv)
    cos, sin = np.cos(freqs).astype(np.float32), np.sin(freqs).astype(np.float32)
    put("cos", np.stack([cos[:, x % 4] for x in r]))
    put("sin", np.stack([sin[:, x % 4] if x % 8 < 4 else -sin[:, x % 4] for x in r]))
    return np.concatenate(parts, axis=1)


CONSTANTS = shape_constants()


class Chip:

    def __init__(self, nc):
        self.nc, self.used = nc, []

    def sem(self, name):
        self.used.append(self.nc.alloc_semaphore(name))
        return self.used[-1]

    def end_stage(self):
        self.nc.clear_and_free_semaphores(self.used)
        self.nc.all_engine_barrier()
        self.used = []


def after(eng, sem, count):
    if not isinstance(count, int) or count > 0:
        eng.wait_ge(sem, count)


def counted(eng, sem):
    at = [0]

    def link(ins):
        at[0] += 1
        ins.then_inc(sem, 1)
        eng.wait_ge(sem, at[0])
    return link


def split_products(nc, out, stat, mov, start, stop):
    (sh, sl), (mh, ml) = stat, mov
    nc.tensor.matmul(out, sh, mh, start=start, stop=False)
    nc.tensor.matmul(out, sh, ml, start=False, stop=False)
    return nc.tensor.matmul(out, sl, mh, start=False, stop=stop)


def load_constants(nc, chip, dram):
    with ExitStack() as ctx:
        loaded = chip.sem("loaded")
        block = ctx.enter_context(nc.Block())

        @block.sync
        def _(sp):
            sp.dma_start(chip.x[:, :, :], dram["x"].rearrange("n p c -> p n c")).then_inc(loaded, 16)
            sp.dma_start(chip.const[:, :], dram["constants"]).then_inc(loaded, 16)
            sp.wait_ge(loaded, 32)


def norm_stage(nc, chip, x, y, yT, weights, products=None, affine=None, twice=False, tag=""):
    with ExitStack() as ctx:
        def sb(name, shape, dt=F32):
            return ctx.enter_context(nc.sbuf_tensor(name + tag, shape, dt))

        def sem(name):
            return chip.sem(name + tag)
        stats, mv = sb("stats", [P, NT, 6]), sb("mv", [P, NT, 2])
        var, std, rstd = sb("var", [P, NT]), sb("std", [P, NT]), sb("rstd", [P, NT])
        z = sb("z", [P, NT, D]) if twice else y
        ps = [ctx.enter_context(nc.psum_tensor(f"tr{i}{tag}", [P, BANK], F32)) for i in range(4)]
        chain, var_ready, std_ready, y_ready = (
            sem("norm_" + n) for n in ("chain", "var_ready", "std_ready", "y_ready"))
        turned, loaded = sem("norm_turned"), sem("norm_loaded")
        block = ctx.enter_context(nc.Block())
        rounds = [(x, y), (y, z)] if twice else [(x, y)]

        @block.sync
        def _(sp):
            for tile, view in weights:
                sp.dma_start(tile, view).then_inc(loaded, 16)
            if weights:
                sp.wait_ge(loaded, 16 * len(weights))

        @block.vector
        def _(dve):
            link = counted(dve, chain)
            for k, (src, dst) in enumerate(rounds):
                for n in range(NT):
                    link(nc.vector.bn_stats(stats[:, n, :], src[:, n, :]))
                for n in range(NT):
                    link(nc.vector.bn_aggr(mv[:, n, :], stats[:, n, :]))
                nc.vector.tensor_scalar_add(var[:, :], mv[:, :, 1], EPS_LN).then_inc(var_ready, 1)
                dve.wait_ge(std_ready, k + 1)
                link(nc.vector.reciprocal(rstd[:, :], std[:, :]))
                for n in range(NT):
                    ins = nc.vector.tensor_scalar(dst[:, n, :], src[:, n, :], mv[:, n, 0:1], rstd[:, n:n + 1],
                                                  ALU.subtract, ALU.mult)
                    if k == len(rounds) - 1:
                        ins.then_inc(y_ready, 1)
                    else:
                        link(ins)

        @block.scalar
        def _(act):
            for k in range(len(rounds)):
                act.wait_ge(var_ready, k + 1)
                nc.scalar.activation(std[:, :], var[:, :], ACT.Sqrt).then_inc(std_ready, 1)
            if affine is not None and weights:
                act.wait_ge(loaded, 16 * len(weights))
            for q in range(2):
                for h in range(HALVES):
                    act.wait_ge(turned, 2 * q + h + 1)
                    src = ps[2 * q + h][:, :]
                    if affine is None:
                        nc.scalar.activation(yT(h, q), src, ACT.Copy)
                    else:
                        nc.scalar.activation(yT(h, q), src.rearrange("p (b t) -> p b t", t=T), ACT.Identity,
                                             scale=affine[0][:, h:h + 1], bias=affine[1][:, h:h + 1])

        @block.tensor
        def _(pe):
            for q in range(2):
                for n in range(4 * q, 4 * q + 4):
                    pe.wait_ge(y_ready, n + 1)
                    for h in range(HALVES):
                        ins = nc.tensor.transpose(ps[2 * q + h][:, P * (n % 4):P * (n % 4) + P],
                                                  z[:, n, P * h:P * h + P], chip.ident)
                        if n % 4 == 3:
                            ins.then_inc(turned, 1)


def chan(w):
    return w.rearrange("(c p) n -> p c n", p=P)


def query_stage(nc, chip, yT, wq, bq, scale, qT, wk, wv, split, tag):
    with ExitStack() as ctx:
        ps = [ctx.enter_context(nc.psum_tensor(f"q{i}{tag}", [P, BANK], F32)) for i in range(4)]
        done, chain, chain2 = [chip.sem(n + tag) for n in ("q_done", "w_hi", "w_hi2")]
        block = ctx.enter_context(nc.Block())

        @block.tensor
        def _(pe):
            for h in range(HALVES):
                for q in range(2):
                    for c in range(HALVES):
                        ins = nc.tensor.matmul(ps[2 * h + q][:, :], wq[:, c, P * h:P * h + P],
                                               yT[:, c, BANK * q:BANK * q + BANK], start=c == 0, stop=c == 1)
                    ins.then_inc(done, 1)

        @block.vector
        def _(dve):
            for h in range(HALVES):
                for q in range(2):
                    dve.wait_ge(done, 2 * h + q + 1)
                    nc.vector.tensor_scalar(qT[:, h, BANK * q:BANK * q + BANK], ps[2 * h + q][:, :],
                                            bq[:, h:h + 1], scale, ALU.add, ALU.mult)

        @block.gpsimd
        def _(pool):
            link = counted(pool, chain)
            for w, (hi, lo) in zip((wk, wv), split):
                link(nc.gpsimd.tensor_copy(hi[:, :, :], w[:, :, :]))
                nc.gpsimd.tensor_tensor(lo[:, :, :], w[:, :, :], hi[:, :, :].bitcast(F32), ALU.subtract)


def cross_attention(nc, chip, ctxT, qT, attnT, wk, wv, bk, bv, mask, tag):
    masked = mask is not None
    together = 1 if masked else 2
    depth = 2 * together
    with ExitStack() as ctx:
        def sb(name, shape, dt=F32):
            return ctx.enter_context(nc.sbuf_tensor(name + tag, shape, dt))

        def sem(name):
            return chip.sem(name + tag)
        raw = [sb(f"raw{i}", [P, HALVES, BANK]) for i in range(2)]
        xh, xl = sb("ctx_hi", [P, HALVES, KPAD], F32R), sb("ctx_lo", [P, HALVES, KPAD], F32R)
        kh = [sb(f"k_hi{i}", [P, HALVES, KPAD], F32R) for i in range(2)]
        kl = [sb(f"k_lo{i}", [P, HALVES, KPAD], F32R) for i in range(2)]
        v = [sb(f"v{i}", [P, KT, D]) for i in range(2)]
        qh = [sb(f"q_hi{i}", [P, PAIRS, P], F32R) for i in range(2)]
        ql = [sb(f"q_lo{i}", [P, PAIRS, P], F32R) for i in range(2)]
        qf = sb("q_block", [P, 4, P])
        prob = [sb(f"prob{i}", [P, KEYS]) for i in range(2)]
        probT = [sb(f"probT{i}", [P, KT, P]) for i in range(depth)]
        mx2, nm = sb("max_parts", [P, 2, 2]), sb("neg_max", [P, 2])
        sums, rsum, rec = sb("sums", [P, 2, PAIRS, 2]), sb("rsum", [P, PAIRS]), sb("rec", [P, PAIRS])
        recT, spread = sb("recT", [PAIRS, P]), sb("spread", [P, HALVES, 2, T])
        scaled = sb("scaled", [P, HALVES, 2, T])
        if masked:
            mraw = sb("mask_raw", [P, KEYS])
            mb = [sb(f"mask_hi_lo{i}", [P, KPAD], F32R) for i in range(2)]
            pick = sb("pick", [P, P], F32R)
        SC = ctx.enter_context(nc.psum_tensor("scores" + tag, [P, 4 * BANK], F32))
        TR = [ctx.enter_context(nc.psum_tensor(f"turn{i}{tag}", [P, BANK], F32)) for i in range(2)]
        OUT = ctx.enter_context(nc.psum_tensor("values" + tag, [P, BANK], F32))
        PJ = ctx.enter_context(nc.psum_tensor("project" + tag, [P, BANK], F32))

        raw_in = [sem(f"raw_in{i}") for i in range(2)]
        mask_in, mask_ready, mask_step = sem("mask_in"), sem("mask_ready"), sem("mask_step")
        ctx_hi_done, ctx_ready = sem("ctx_hi_done"), sem("ctx_ready")
        q_step, q_ready, pads, waits_passed = sem("q_step"), sem("q_ready"), sem("pads"), sem("waits_passed")
        k_projected, v_projected, k_hi_done, bank_free = (sem("k_projected"), sem("v_projected"),
                                                          sem("k_hi_done"), sem("bank_free"))
        scored_a, scored_b, max_parts, max_ready = sem("scored_a"), sem("scored_b"), sem("max_parts"), sem("max_ready")
        exp_a, exp_b, turned = sem("exp_a"), sem("exp_b"), [sem(f"turned{i}") for i in range(2)]
        moved = [sem(f"moved{i}") for i in range(2)]
        values_done, values_read = sem("values_done"), sem("values_read")
        rec_step, rec_ready, rec_turned, rec_spread, out_step = (sem("rec_step"), sem("rec_ready"),
                                                                 sem("rec_turned"), sem("rec_spread"), sem("out_step"))
        block = ctx.enter_context(nc.Block())

        def width(chunk):
            return min(BANK, KEYS - BANK * chunk)

        def rows(tile):
            return min(P, KEYS - P * tile)

        TILES = [[t for t in range(4 * g, 4 * g + 4) if t < KT] for g in range(4)]

        def J(n, index):
            if isinstance(n, int) and n == 0:
                return 15 + index
            return 17 * n + 13 + index

        def bodies(eng, body, tail):
            body(0, 0)
            with eng.Fori(0, NB // 2 - 1) as i:
                body(2 * i + 1, 1)
                body(2 * i + 2, 0)
            body(NB - 1, 1)
            tail()

        def is_last(n):
            return isinstance(n, int) and n == NB - 1

        def is_first(n):
            return isinstance(n, int) and n == 0

        @block.sync
        def _(sp):
            def loads(m, later):
                if masked:
                    sp.wait_ge(mask_ready, m)
                    for k in range(2):
                        sp.dma_start(mraw[T * k:T * k + T, :],
                                     mask[bass.ds(m, 1), :, :].rearrange("a q k -> (a q) k")).then_inc(mask_in, 16)
                for j in range(4):
                    if later or j >= 2:
                        sp.wait_ge(ctx_ready, 4 * m + j - 1)
                    sp.dma_start(raw[j % 2][:, :, 0:width(j)],
                                 ctxT[bass.ds(m, 1), :, BANK * j:BANK * j + width(j)].rearrange(
                                     "a (c p) k -> p (a c) k", p=P)).then_inc(raw_in[j % 2], 16)
            loads(0, False)
            with sp.Fori(1, NB) as m:
                loads(m, True)

        @block.gpsimd
        def _(pool):
            nc.gpsimd.memset(xh[:, :, KEYS:KPAD].bitcast(F32), 0.0).then_inc(pads, 1)
            nc.gpsimd.memset(xl[:, :, KEYS:KPAD].bitcast(F32), 0.0).then_inc(pads, 1)
            if masked:
                for b in mb:
                    nc.gpsimd.memset(b[:, KEYS:KPAD].bitcast(F32), 0.0).then_inc(pads, 1)
                nc.gpsimd.tensor_copy(pick[:, :], chip.cst("same_query")).then_inc(pads, 1)

            def passed(sem, count):
                pool.wait_ge(sem, count)
                pool.sem_inc(waits_passed, 1)

            def queries(m, par, reuse):
                if reuse:
                    passed(scored_b, 8 * m - 8)
                for h in range(HALVES):
                    block8 = qf[:, :, :].rearrange("p a (b t) -> p (a b) t", t=T)
                    nc.gpsimd.tensor_tensor(
                        block8, qT[:, h:h + 1, bass.ds(T * m, T)].to_broadcast([P, 8, T]),
                        chip.cst("qmask").rearrange("p (a o) -> p a o", o=1).to_broadcast([P, 8, T]),
                        ALU.mult).then_inc(q_step, 1)
                    passed(q_step, 4 * m + 2 * h + 1)
                    nc.gpsimd.tensor_copy(qh[par][:, 4 * h:4 * h + 4, :], qf[:, :, :]).then_inc(q_step, 1)
                    passed(q_step, 4 * m + 2 * h + 2)
                    nc.gpsimd.tensor_tensor(ql[par][:, 4 * h:4 * h + 4, :], qf[:, :, :],
                                            qh[par][:, 4 * h:4 * h + 4, :].bitcast(F32),
                                            ALU.subtract).then_inc(q_ready, 1)
                    passed(q_ready, 2 * m + h + 1)

            def masks(m, par):
                passed(mask_in, 32 * m + 32)
                nc.gpsimd.tensor_scalar(mraw[:, :], mraw[:, :], -1.0e9, None, ALU.mult).then_inc(mask_step, 1)
                passed(mask_step, 2 * m + 1)
                nc.gpsimd.tensor_copy(mb[par][:, 0:KEYS], mraw[:, :]).then_inc(mask_step, 1)
                passed(mask_step, 2 * m + 2)
                nc.gpsimd.tensor_tensor(mb[par][T:P, 0:KEYS], mraw[T:P, :], mb[par][T:P, 0:KEYS].bitcast(F32),
                                        ALU.subtract).then_inc(mask_ready, 1)

            def context(m, reuse):
                for j in range(4):
                    w, cols = width(j), slice(BANK * j, BANK * j + width(j))
                    passed(raw_in[j % 2], 32 * m + 16 * (j // 2) + 16)
                    if reuse:
                        passed(v_projected, 7 * m - 7 + min(2 * j + 2, 7))
                        passed(k_projected, 8 * m - 8 + 2 * j + 2)
                    nc.gpsimd.tensor_copy(xh[:, :, cols], raw[j % 2][:, :, 0:w]).then_inc(ctx_hi_done, 1)
                    passed(ctx_hi_done, 4 * m + j + 1)
                    nc.gpsimd.tensor_tensor(xl[:, :, cols], raw[j % 2][:, :, 0:w], xh[:, :, cols].bitcast(F32),
                                            ALU.subtract).then_inc(ctx_ready, 1)

            context(0, False)
            queries(0, 0, False)
            if masked:
                masks(0, 0)
            context(1, True)

            def body(n, par):
                if is_last(n):
                    return
                queries(n + 1, 1 - par, True)
                if masked:
                    masks(n + 1, 1 - par)
                if not (isinstance(n, int) and n + 2 >= NB):
                    context(n + 2, True)
            body(0, 0)
            with pool.Fori(0, NB // 2 - 2) as i:
                body(2 * i + 1, 1)
                body(2 * i + 2, 0)
            body(NB - 3, 1)
            body(NB - 2, 0)

        @block.tensor
        def _(pe):
            def k_unit(n, p, uses):
                chunk, h = p // 2, p % 2
                w = width(chunk) + (width(chunk) & 1)
                pe.wait_ge(ctx_ready, 4 * n + chunk + 1)
                if uses is not None:
                    pe.wait_ge(bank_free, uses)
                for c in range(HALVES):
                    cols, outs = slice(BANK * chunk, BANK * chunk + w), slice(P * h, P * h + P)
                    ins = split_products(nc, PJ[:, 0:w], (wk[0][:, c, outs], wk[1][:, c, outs]),
                                         (xh[:, c, cols], xl[:, c, cols]), c == 0, c == 1)
                ins.then_inc(k_projected, 1)

            def v_unit(n, u, uses):
                pe.wait_ge(ctx_ready, 4 * n + u // 2 + 1)
                pe.wait_ge(bank_free, uses)
                for t in range(2 * u, min(2 * u + 2, KT)):
                    cols = slice(P * t, P * t + rows(t))
                    for c in range(HALVES):
                        ins = split_products(nc, PJ[0:rows(t), D * (t % 2):D * (t % 2) + D],
                                             (xh[:, c, cols], xl[:, c, cols]),
                                             (wv[0][:, c, :], wv[1][:, c, :]), c == 0, c == 1)
                ins.then_inc(v_projected, 1)

            def scores(n, p, par):
                h = p // 4
                for j in range(4):
                    if j % 2 == 0:
                        pe.wait_ge(exp_b if j else exp_a, 8 * n + p)
                    w = width(j) + (width(j) & 1)
                    cols, out = slice(BANK * j, BANK * j + w), SC[:, BANK * j:BANK * j + w]
                    ins = split_products(nc, out, (qh[par][:, p, :], ql[par][:, p, :]),
                                         (kh[par][:, h, cols], kl[par][:, h, cols]), True, not masked)
                    if masked:
                        ins = nc.tensor.matmul(out, pick[:, :], mb[par][:, cols], start=False, stop=True)
                    if j % 2:
                        ins.then_inc(scored_b if j == 3 else scored_a, 1)

            def turn(pairs, p, groups):
                if groups[0] == 0:
                    pe.wait_ge(exp_b, pairs + 1)
                for g in groups:
                    pe.wait_ge(moved[g % 2], 2 * pairs + g // 2)
                    for t in TILES[g]:
                        ins = nc.tensor.transpose(TR[g % 2][0:rows(t), P * (t % 4):P * (t % 4) + P],
                                                  prob[p % 2][:, P * t:P * t + rows(t)], chip.ident)
                    ins.then_inc(turned[g % 2], 1)

            def values(n, pairs, p, par):
                if p == 0:
                    pe.wait_ge(values_read, n)
                pe.wait_ge(moved[0], 2 * pairs + 2 * together)
                pe.wait_ge(moved[1], 2 * pairs + 2 * together)
                for t in range(KT):
                    for i in range(p, p + together):
                        ins = nc.tensor.matmul(OUT[PW * (i % 4):PW * (i % 4) + PW, P * (i // 4):P * (i // 4) + P],
                                               v[par][0:rows(t), t, PW * i:PW * i + PW], probT[i % depth][0:rows(t), t, :],
                                               start=t == 0, stop=t == KT - 1)
                        if t == KT - 1:
                            ins.then_inc(values_done, 1)

            def reciprocals(n, uses):
                pe.wait_ge(rec_ready, n)
                pe.wait_ge(bank_free, uses)
                nc.tensor.transpose(PJ[0:PAIRS, 0:P], rec[:, :], chip.ident).then_inc(rec_turned, 1)

            def spreads(uses):
                pe.wait_ge(bank_free, uses)
                for h in range(HALVES):
                    ins = nc.tensor.matmul(PJ[:, P * h:P * h + P],
                                           chip.cst("pair_to_channels")[0:PAIRS, P * h:P * h + P], recT[:, :],
                                           start=True, stop=True)
                ins.then_inc(rec_spread, 1)

            if masked:
                pe.wait_ge(pads, 5)
            else:
                pe.wait_ge(pads, 2)
            for p in range(PAIRS):
                k_unit(0, p, p if p else None)
            for u in range(7):
                v_unit(0, u, 8 + u)

            def body(n, par):
                first, last = is_first(n), is_last(n)
                pe.wait_ge(q_ready, 2 * n + 2)
                if masked:
                    pe.wait_ge(mask_ready, n + 1)
                pe.wait_ge(bank_free, J(n, 0))
                for p in range(PAIRS):
                    at = 8 * n + p
                    scores(n, p, par)
                    if p == 0:
                        if not first:
                            reciprocals(n, J(n, 0))
                            turn(at - 1, 7, [0, 1])
                            if together == 1:
                                values(n - 1, at - 2, 6, 1 - par)
                            turn(at - 1, 7, [2, 3])
                        if not last:
                            k_unit(n + 1, 0, J(n, 0 if first else 1))
                    elif p == 1:
                        if not first:
                            spreads(J(n, 1 if last else 2))
                        turn(at - 1, 0, [0, 1])
                        if not first and together == 1:
                            values(n - 1, at - 2, 7, 1 - par)
                        elif not first:
                            values(n - 1, at - 3, 6, 1 - par)
                        turn(at - 1, 0, [2, 3])
                        if not last:
                            v_unit(n + 1, 0, J(n, 1 if first else 3))
                            k_unit(n + 1, 1, J(n, 2 if first else 4))
                    else:
                        turn(at - 1, p - 1, [0, 1])
                        if not last:
                            v_unit(n + 1, p - 1, J(n, 2 * p - 1 if first else 2 * p + 1))
                        if together == 1:
                            values(n, at - 2, p - 2, par)
                        elif p % 2:
                            values(n, at - 3, p - 3, par)
                        turn(at - 1, p - 1, [2, 3])
                        if not last:
                            k_unit(n + 1, p, J(n, 2 * p if first else 2 * p + 2))

            def tail():
                pairs = PAIRS * NB
                reciprocals(NB, J(NB - 1, 2))
                turn(pairs - 1, 7, [0, 1])
                if together == 1:
                    values(NB - 1, pairs - 2, 6, 1)
                turn(pairs - 1, 7, [2, 3])
                spreads(J(NB - 1, 3))
                values(NB - 1, pairs - together, PAIRS - together, 1)
            bodies(pe, body, tail)

        @block.scalar
        def _(act):
            def k_hi(n, p, par):
                chunk, h = p // 2, p % 2
                w = width(chunk) + (width(chunk) & 1)
                act.wait_ge(k_projected, 8 * n + p + 1)
                nc.scalar.activation(kh[par][:, h, BANK * chunk:BANK * chunk + w], PJ[:, 0:w], ACT.Identity,
                                     bias=bk[:, h:h + 1]).then_inc(k_hi_done, 1)

            def v_copy(n, u, par):
                act.wait_ge(v_projected, 7 * n + u + 1)
                tiles = min(2, KT - 2 * u)
                r = rows(2 * u)
                nc.scalar.activation(v[par][0:r, 2 * u:2 * u + tiles, :],
                                     PJ[0:r, 0:D * tiles].rearrange("p (a c) -> p a c", c=D),
                                     ACT.Copy).then_inc(bank_free, 1)

            for p in range(PAIRS):
                k_hi(0, p, 0)
            for u in range(7):
                v_copy(0, u, 0)

            def body(n, par):
                for p in range(PAIRS):
                    if p >= 2 and not is_last(n):
                        v_copy(n + 1, p - 1, 1 - par)
                    act.wait_ge(max_ready, 8 * n + p + 1)
                    for lo, hi, k, done in ((0, 2 * BANK, 0, exp_a), (2 * BANK, KEYS, 1, exp_b)):
                        nc.scalar.activation(prob[p % 2][:, lo:hi], SC[:, lo:hi], ACT.Exp, bias=nm[:, p % 2:p % 2 + 1],
                                             accum_out=sums[:, par, p, k:k + 1]).then_inc(done, 1)
                    if not is_last(n):
                        if p == 1:
                            v_copy(n + 1, 0, 1 - par)
                        k_hi(n + 1, p, 1 - par)
            bodies(act, body, lambda: None)

        @block.vector
        def _(dve):
            def k_lo(n, p, par):
                chunk, h = p // 2, p % 2
                w = width(chunk) + (width(chunk) & 1)
                cols = slice(BANK * chunk, BANK * chunk + w)
                dve.wait_ge(k_hi_done, 8 * n + p + 1)
                nc.vector.scalar_tensor_tensor(kl[par][:, h, cols], PJ[:, 0:w], bk[:, h:h + 1],
                                               kh[par][:, h, cols].bitcast(F32), ALU.add,
                                               ALU.subtract).then_inc(bank_free, 1)

            def move(pairs, p):
                for g in range(4):
                    r, tiles = rows(TILES[g][0]), len(TILES[g])
                    dve.wait_ge(turned[g % 2], 2 * pairs + g // 2 + 1)
                    nc.vector.tensor_copy(probT[p % depth][0:r, 4 * g:4 * g + tiles, :],
                                          TR[g % 2][0:r, 0:P * tiles].rearrange("p (a c) -> p a c", c=P)
                                          ).then_inc(moved[g % 2], 1)

            def take_reciprocals(n, par):
                dve.wait_ge(exp_b, 8 * n)
                nc.vector.tensor_reduce(rsum[:, :], sums[:, par, :, :], AX.X, ALU.add).then_inc(rec_step, 1)
                dve.wait_ge(rec_step, n)
                nc.vector.reciprocal(rec[:, :], rsum[:, :]).then_inc(rec_ready, 1)

            def keep_turned(n):
                dve.wait_ge(rec_turned, n)
                nc.vector.tensor_copy(recT[:, :], PJ[0:PAIRS, 0:P]).then_inc(bank_free, 1)

            def keep_spread(n):
                dve.wait_ge(rec_spread, n)
                own = chip.cst("head_of_pair")
                bank = PJ[:, 0:2 * P].rearrange("p (h a t) -> p h a t", h=2, a=2)
                nc.vector.tensor_scalar(spread[:, :, 0, :], bank[:, :, 0, :], own[:, 0:1], None,
                                        ALU.mult).then_inc(out_step, 1)
                nc.vector.tensor_scalar(spread[:, :, 1, :], bank[:, :, 1, :], own[:, 1:2], None,
                                        ALU.mult).then_inc(bank_free, 1)

            def finish(n, uses):
                dve.wait_ge(values_done, 8 * n)
                dve.wait_ge(out_step, 2 * n - 1)
                dve.wait_ge(bank_free, uses)
                nc.vector.tensor_tensor(scaled[:, :, :, :].rearrange("p h a t -> p (h a t)"), OUT[:, 0:2 * P],
                                        spread[:, :, :, :].rearrange("p h a t -> p (h a t)"),
                                        ALU.mult).then_inc(values_read, 1)
                dve.wait_ge(values_read, n)
                for h in range(HALVES):
                    ins = nc.vector.scalar_tensor_tensor(attnT[:, h, bass.ds(T * (n - 1), T)], scaled[:, h, 0, :],
                                                         bv[:, h:h + 1], scaled[:, h, 1, :], ALU.add, ALU.add)
                ins.then_inc(out_step, 1)

            for p in range(PAIRS):
                k_lo(0, p, 0)

            def body(n, par):
                first, last = is_first(n), is_last(n)
                for p in range(PAIRS):
                    at, b = 8 * n + p, p % 2
                    dve.wait_ge(scored_a, at + 1)
                    nc.vector.reduce_max(mx2[:, b, 0:1], SC[:, 0:2 * BANK], AX.X).then_inc(max_parts, 1)
                    dve.wait_ge(scored_b, at + 1)
                    nc.vector.reduce_max(mx2[:, b, 1:2], SC[:, 2 * BANK:KEYS], AX.X).then_inc(max_parts, 1)
                    dve.wait_ge(max_parts, 2 * at + 2)
                    nc.vector.tensor_reduce(nm[:, b:b + 1], mx2[:, b, :], AX.X, ALU.max, negate=True
                                            ).then_inc(max_ready, 1)
                    if p == 0 and not first:
                        take_reciprocals(n, 1 - par)
                        keep_turned(n)
                    if p == 1 and not first:
                        keep_spread(n)
                    if p >= 1 or not first:
                        move(at - 1, (p + 7) % 8)
                    if p == 1 and not first:
                        finish(n, J(n, 2 if last else 3))
                    if not last:
                        k_lo(n + 1, p, 1 - par)

            def tail():
                take_reciprocals(NB, 1)
                keep_turned(NB)
                move(PAIRS * NB - 1, 7)
                keep_spread(NB)
                finish(NB, J(NB - 1, 4))
            bodies(dve, body, tail)


def output_stage(nc, chip, attnT, wo, bo_row, tag):
    with ExitStack() as ctx:
        ps = [ctx.enter_context(nc.psum_tensor(f"o{i}{tag}", [P, BANK], F32)) for i in range(4)]
        done, ones_set = chip.sem("o_done" + tag), chip.sem("ones" + tag)
        ones = ctx.enter_context(nc.sbuf_tensor("ones" + tag, [1, P], F32))
        block = ctx.enter_context(nc.Block())

        @block.tensor
        def _(pe):
            pe.wait_ge(ones_set, 1)
            for n in range(NT):
                out = ps[n // 2][:, D * (n % 2):D * (n % 2) + D]
                for c in range(HALVES):
                    ins = nc.tensor.matmul(out, attnT[:, c, P * n:P * n + P], wo[:, c, :], start=c == 0,
                                           stop=c == 1 and bo_row is None)
                if bo_row is not None:
                    ins = nc.tensor.matmul(out, ones[:, :], bo_row, start=False, stop=True)
                if n % 2:
                    ins.then_inc(done, 1)

        @block.vector
        def _(dve):
            nc.vector.memset(ones[:, :], 1.0).then_inc(ones_set, 1)
            for q in range(NT // 2):
                dve.wait_ge(done, q + 1)
                nc.vector.tensor_tensor(chip.x[:, 2 * q:2 * q + 2, :],
                                        chip.x[:, 2 * q:2 * q + 2, :],
                                        ps[q][:, :].rearrange("p (a c) -> p a c", c=D), ALU.add)


def rwkv_stage(nc, chip, dram, tag):
    F = 4 * D
    FC = F // P
    with ExitStack() as ctx:
        def sb(name, shape, dt=F32):
            return ctx.enter_context(nc.sbuf_tensor(name + tag, shape, dt))
        y, shifted = sb("y", [P, NT, D]), sb("shifted", [P, HALVES, NB, T + 1])
        cols = {n: sb(n, [P, HALVES]) for n in ("ln1_g", "ln1_b", "ln2_g", "ln2_b", "time_first")}
        mixes = sb("mixes", [P, 5, HALVES])
        wt = {n: sb(n, [P, HALVES, D]) for n in ("Wk_t", "Wv_t", "Wr_t", "Wr_c")}
        wkc, wvc = sb("Wk_c", [P, HALVES, F]), sb("Wv_c", [P, FC, D])
        with nc.Block() as block:
            @block.vector
            def _(dve):
                nc.vector.memset(shifted[:, :, :, 0:1], 0.0)
        weights = [(t[:, :], dram["L0_attn_" + n]) for n, t in cols.items()]
        weights += [(mixes[:, i, :], dram["L0_attn_" + n])
                    for i, n in enumerate(("mix_k", "mix_v", "mix_r", "cmix_k", "cmix_r"))]
        weights += [(t[:, :, :], chan(dram["L0_attn_" + n])) for n, t in wt.items()]
        weights += [(wkc[:, :, :], chan(dram["L0_attn_Wk_c"])), (wvc[:, :, :], chan(dram["L0_attn_Wv_c"]))]

        def target(h, q):
            return shifted[:, h, NB // 2 * q:NB // 2 * q + NB // 2, 1:T + 1]
        norm_stage(nc, chip, chip.x, y, target, weights, affine=(cols["ln1_g"], cols["ln1_b"]), twice=True, tag=tag)
        time_mix(nc, chip, y, shifted, mixes, cols["time_first"], wt, tag)
        with nc.sbuf_tensor("z2" + tag, [P, NT, D], F32) as z:
            norm_stage(nc, chip, y, z, target, [], affine=(cols["ln2_g"], cols["ln2_b"]), tag=tag + "2")
        channel_mix(nc, chip, y, shifted, mixes, wt["Wr_c"], wkc, wvc, tag)


def mix_tokens(nc, eng, link, shifted, mixes, rest, i, mixed, part):
    for h in range(HALVES):
        now, before = shifted[:, h, :, 1:T + 1], shifted[:, h, :, 0:T]
        view = mixed[:, h, :].rearrange("p (b t) -> p b t", t=T)
        link(nc.vector.tensor_scalar(part[:, :, :], before, rest[:, i, h:h + 1], None, ALU.mult))
        link(nc.vector.scalar_tensor_tensor(view, now, mixes[:, i, h:h + 1], part[:, :, :], ALU.mult, ALU.add))


def time_mix(nc, chip, y, shifted, mixes, first, wt, tag):
    EPS = 1e-8
    with ExitStack() as ctx:
        def sb(name, shape, dt=F32):
            return ctx.enter_context(nc.sbuf_tensor(name + tag, shape, dt))

        def sem(name):
            return chip.sem(name + tag)
        rest = sb("rest", [P, 5, HALVES])
        mixed, part = [sb(f"mixed{i}", [P, HALVES, TOK]) for i in range(3)], sb("part", [P, NB, T])
        kvr = [sb(n, [P, HALVES, TOK]) for n in ("k", "v", "r")]
        restart = sb("restart", [P, TOK])
        m, gap, e, s = [sb(n, [P, TOK]) for n in ("m", "gap", "e", "s")]
        pp = sb("pp", [P, NB, T + 1])
        p2, a, b, aa, e1, e2 = [sb(n, [P, TOK]) for n in ("p2", "a", "b", "aa", "e1", "e2")]
        ps = [ctx.enter_context(nc.psum_tensor(f"tm{i}{tag}", [P, BANK], F32)) for i in range(8)]
        chain, mixed_ready, projected, kept = sem("chain"), sem("mixed_ready"), sem("projected"), sem("kept")
        e_in, gap_in, s_in, a_in, b_in, e1_in, e2_in = [sem(n + "_in") for n in ("e", "gap", "s", "a", "b", "e1", "e2")]
        e_out, gap_out, s_out, a_out, b_out, e1_out, e2_out = [sem(n + "_out") for n in
                                                               ("e", "gap", "s", "a", "b", "e1", "e2")]
        wkv_ready, wkv_turned = sem("wkv_ready"), sem("wkv_turned")
        block = ctx.enter_context(nc.Block())

        def seq(t):
            return t.rearrange("p (b t) -> p b t", t=T)

        @block.vector
        def _(dve):
            link = counted(dve, chain)
            link(nc.vector.tensor_scalar(rest[:, :, :], mixes[:, :, :], -1.0, 1.0, ALU.mult, ALU.add))
            for i in range(3):
                mix_tokens(nc, dve, link, shifted, mixes, rest, i, mixed[i], part)
                nc.vector.engine_nop().then_inc(mixed_ready, 1)
            nc.vector.tensor_copy(seq(restart[:, :]), chip.cst("restart").rearrange("p (o t) -> p o t", o=1)
                                  .to_broadcast([P, NB, T]))
            nc.vector.memset(pp[:, :, 0:1], NEG)
            link(nc.vector.memset(seq(gap[:, :])[:, :, 0:1], NEG))
            for h in range(HALVES):
                k, v, r = [t[:, h, :] for t in kvr]
                before = pp[:, :, 0:T]
                dve.wait_ge(kept, 2 * h + 2)
                link(nc.vector.tensor_tensor_scan(m[:, :], restart[:, :], k, NEG, ALU.add, ALU.max))
                nc.vector.tensor_tensor(e[:, :], k, m[:, :], ALU.subtract).then_inc(e_in, 1)
                if h:
                    link(nc.vector.memset(seq(gap[:, :])[:, :, 0:1], NEG))
                nc.vector.tensor_tensor(seq(gap[:, :])[:, :, 1:T], seq(m[:, :])[:, :, 0:T - 1],
                                        seq(m[:, :])[:, :, 1:T], ALU.subtract).then_inc(gap_in, 1)
                dve.wait_ge(e_out, h + 1)
                link(nc.vector.tensor_scalar_add(e[:, :], e[:, :], EPS))
                dve.wait_ge(gap_out, h + 1)
                nc.vector.tensor_tensor_scan(s[:, :], gap[:, :], e[:, :], 0.0, ALU.mult, ALU.add).then_inc(s_in, 1)
                dve.wait_ge(s_out, h + 1)
                link(nc.vector.tensor_tensor(pp[:, :, 1:T + 1], seq(s[:, :]), seq(m[:, :]), ALU.add))
                link(nc.vector.tensor_tensor(seq(p2[:, :]), before, seq(k), ALU.max))
                nc.vector.tensor_tensor(seq(a[:, :]), before, seq(p2[:, :]), ALU.subtract).then_inc(a_in, 1)
                nc.vector.tensor_tensor(b[:, :], k, p2[:, :], ALU.subtract).then_inc(b_in, 1)
                dve.wait_ge(b_in, h + 1)
                link(nc.vector.scalar_tensor_tensor(seq(p2[:, :]), seq(k), first[:, h:h + 1], before,
                                                    ALU.add, ALU.max))
                nc.vector.tensor_tensor(seq(e1[:, :]), before, seq(p2[:, :]), ALU.subtract).then_inc(e1_in, 1)
                nc.vector.scalar_tensor_tensor(e2[:, :], k, first[:, h:h + 1], p2[:, :], ALU.add,
                                               ALU.subtract).then_inc(e2_in, 1)
                dve.wait_ge(kept, 4 + 2 * h + 2)
                dve.wait_ge(a_out, h + 1)
                dve.wait_ge(b_out, h + 1)
                link(nc.vector.tensor_tensor(b[:, :], b[:, :], v, ALU.mult))
                link(nc.vector.tensor_tensor_scan(aa[:, :], a[:, :], b[:, :], 0.0, ALU.mult, ALU.add))
                dve.wait_ge(e1_out, h + 1)
                dve.wait_ge(e2_out, h + 1)
                link(nc.vector.scalar_tensor_tensor(p2[:, :], e1[:, :], EPS, e2[:, :], ALU.add, ALU.add))
                link(nc.vector.reciprocal(p2[:, :], p2[:, :]))
                link(nc.vector.tensor_tensor(b[:, :], e2[:, :], v, ALU.mult))
                link(nc.vector.tensor_tensor(seq(a[:, :])[:, :, 1:T], seq(e1[:, :])[:, :, 1:T],
                                             seq(aa[:, :])[:, :, 0:T - 1], ALU.mult))
                link(nc.vector.tensor_tensor(seq(b[:, :])[:, :, 1:T], seq(b[:, :])[:, :, 1:T],
                                             seq(a[:, :])[:, :, 1:T], ALU.add))
                dve.wait_ge(kept, 8 + 2 * h + 2)
                link(nc.vector.tensor_tensor(p2[:, :], p2[:, :], r, ALU.mult))
                nc.vector.tensor_tensor(r, b[:, :], p2[:, :], ALU.mult).then_inc(wkv_ready, 1)
            for q in range(NT // 2):
                dve.wait_ge(wkv_turned, q + 1)
                rows = y[:, 2 * q:2 * q + 2, :]
                nc.vector.tensor_tensor(rows, rows, ps[q][:, :].rearrange("p (a c) -> p a c", c=D), ALU.add)

        @block.tensor
        def _(pe):
            for i, n in enumerate(("Wk_t", "Wv_t", "Wr_t")):
                pe.wait_ge(mixed_ready, i + 1)
                for h in range(HALVES):
                    for q in range(2):
                        bank = 4 * (i % 2) + 2 * h + q
                        if i == 2:
                            pe.wait_ge(kept, 2 * h + q + 1)
                        for c in range(HALVES):
                            ins = nc.tensor.matmul(ps[bank][:, :], wt[n][:, c, P * h:P * h + P],
                                                   mixed[i][:, c, BANK * q:BANK * q + BANK], start=c == 0, stop=c == 1)
                        ins.then_inc(projected, 1)
            pe.wait_ge(kept, 12)
            for h in range(HALVES):
                pe.wait_ge(wkv_ready, h + 1)
                for n in range(NT):
                    ins = nc.tensor.transpose(ps[n // 2][:, D * (n % 2) + P * h:D * (n % 2) + P * h + P],
                                              kvr[2][:, h, P * n:P * n + P], chip.ident)
                    if h and n % 2:
                        ins.then_inc(wkv_turned, 1)

        @block.scalar
        def _(act):
            for i in range(3):
                for h in range(HALVES):
                    for q in range(2):
                        act.wait_ge(projected, 4 * i + 2 * h + q + 1)
                        nc.scalar.activation(kvr[i][:, h, BANK * q:BANK * q + BANK],
                                             ps[4 * (i % 2) + 2 * h + q][:, :],
                                             ACT.Sigmoid if i == 2 else ACT.Copy).then_inc(kept, 1)
            for h in range(HALVES):
                for t, before, f, after in ((e, e_in, ACT.Exp, e_out), (gap, gap_in, ACT.Exp, gap_out),
                                            (s, s_in, ACT.Ln, s_out), (a, a_in, ACT.Exp, a_out),
                                            (b, b_in, ACT.Exp, b_out), (e1, e1_in, ACT.Exp, e1_out),
                                            (e2, e2_in, ACT.Exp, e2_out)):
                    act.wait_ge(before, h + 1)
                    nc.scalar.activation(t[:, :], t[:, :], f).then_inc(after, 1)


def channel_mix(nc, chip, y, shifted, mixes, wrc, wkc, wvc, tag):
    FC = wvc.shape[1]
    with ExitStack() as ctx:
        def sb(name, shape, dt=F32):
            return ctx.enter_context(nc.sbuf_tensor(name + tag, shape, dt))

        def sem(name):
            return chip.sem(name + tag)
        rest, part = sb("crest", [P, 5, HALVES]), sb("cpart", [P, NB, T])
        mixed = [sb(f"cmixed{i}", [P, HALVES, TOK]) for i in range(2)]
        hidden, gate = sb("hidden", [P, FC, TOK]), sb("gate", [P, NT, D])
        pk = [ctx.enter_context(nc.psum_tensor(f"ck{i}{tag}", [P, BANK], F32)) for i in range(4)]
        pv = [ctx.enter_context(nc.psum_tensor(f"cv{i}{tag}", [P, BANK], F32)) for i in range(4)]
        chain, mixed_ready, up, relu, squared = (sem("cchain"), sem("cmixed_ready"), sem("up"), sem("relu"),
                                                 sem("squared"))
        gated, gate_ready, down = sem("gated"), sem("gate_ready"), sem("down")
        block = ctx.enter_context(nc.Block())

        @block.vector
        def _(dve):
            link = counted(dve, chain)
            link(nc.vector.tensor_scalar(rest[:, :, :], mixes[:, :, :], -1.0, 1.0, ALU.mult, ALU.add))
            for i in range(2):
                mix_tokens(nc, dve, link, shifted, mixes, rest, 3 + i, mixed[i], part)
                nc.vector.engine_nop().then_inc(mixed_ready, 1)
            for n in range(NT):
                link(nc.vector.tensor_tensor(chip.x[:, n, :], chip.x[:, n, :], y[:, n, :], ALU.add))
            for n in range(NT):
                dve.wait_ge(gate_ready, n // 2 + 1)
                dve.wait_ge(down, 2 * (n // 2) + 2)
                link(nc.vector.tensor_tensor(gate[:, n, :], gate[:, n, :], pv[n // 2][:, D * (n % 2):D * (n % 2) + D],
                                             ALU.mult))
                nc.vector.tensor_tensor(chip.x[:, n, :], chip.x[:, n, :], gate[:, n, :], ALU.add)

        @block.tensor
        def _(pe):
            pe.wait_ge(mixed_ready, 1)
            for q in range(2):
                for f in range(FC):
                    u = FC * q + f
                    if u >= 4:
                        pe.wait_ge(relu, u - 3)
                    for c in range(HALVES):
                        ins = nc.tensor.matmul(pk[u % 4][:, :], wkc[:, c, P * f:P * f + P],
                                               mixed[0][:, c, BANK * q:BANK * q + BANK], start=c == 0, stop=c == 1)
                    ins.then_inc(up, 1)
            pe.wait_ge(mixed_ready, 2)
            for n in range(NT):
                for c in range(HALVES):
                    ins = nc.tensor.matmul(pv[n // 2][:, D * (n % 2):D * (n % 2) + D], mixed[1][:, c, P * n:P * n + P],
                                           wrc[:, c, :], start=c == 0, stop=c == 1)
                if n % 2:
                    ins.then_inc(gated, 1)
            for n in range(NT):
                if n % 4 == 0:
                    pe.wait_ge(squared, FC * (n // 4 + 1))
                pe.wait_ge(gate_ready, n // 2 + 1)
                for f in range(FC):
                    ins = nc.tensor.matmul(pv[n // 2][:, D * (n % 2):D * (n % 2) + D], hidden[:, f, P * n:P * n + P],
                                           wvc[:, f, :], start=f == 0, stop=f == FC - 1)
                ins.then_inc(down, 1)

        @block.scalar
        def _(act):
            for u in range(2 * FC):
                act.wait_ge(up, u + 1)
                q, f = u // FC, u % FC
                nc.scalar.activation(hidden[:, f, BANK * q:BANK * q + BANK], pk[u % 4][:, :], ACT.Relu).then_inc(relu, 1)
            for i in range(4):
                act.wait_ge(gated, i + 1)
                nc.scalar.activation(gate[:, 2 * i:2 * i + 2, :], pv[i][:, :].rearrange("p (a c) -> p a c", c=D),
                                     ACT.Sigmoid).then_inc(gate_ready, 1)

        @block.gpsimd
        def _(pool):
            for u in range(2 * FC):
                pool.wait_ge(relu, u + 1)
                t = hidden[:, u % FC, BANK * (u // FC):BANK * (u // FC) + BANK]
                nc.gpsimd.tensor_tensor(t, t, t, ALU.mult).then_inc(squared, 1)


def experts_stage(nc, chip, dram, tag):
    E, F = 8, 1024
    FC = F // P
    w1_d, w2_d, b1_d = dram["L0_ffn_W1"], dram["L0_ffn_W2"], dram["L0_ffn_b1"]
    with ExitStack() as ctx:
        def sb(name, shape, dt=F32):
            return ctx.enter_context(nc.sbuf_tensor(name + tag, shape, dt))

        def sem(name):
            return chip.sem(name + tag)
        yh, yl = sb("y_hi", [P, HALVES, TOK], F32R), sb("y_lo", [P, HALVES, TOK], F32R)
        gate, b2 = sb("gate", [P, NT, E]), sb("b2", [E, D])
        w1r, w2r = sb("w1_raw", [P, HALVES, F]), sb("w2_raw", [P, FC, D])
        b1 = [sb(f"b1_{i}", [P, FC]) for i in range(2)]
        w1 = [[sb(f"w1_{n}{i}", [P, HALVES, F], F32R) for n in ("hi", "lo")] for i in range(2)]
        with ExitStack() as ctx2:
            y, yT, wr = [ctx2.enter_context(nc.sbuf_tensor(n + tag, [P, *s], F32)) for n, s in
                         (("y", [NT, D]), ("yT", [HALVES, TOK]), ("wr", [HALVES, E]))]
            norm_stage(nc, chip, chip.x, y, lambda h, q: yT[:, h, BANK * q:BANK * q + BANK],
                       [(wr[:, :, :], chan(dram["L0_ffn_Wr"])), (b2[:, :], dram["L0_ffn_b2"])], tag=tag)
            route(nc, chip, yT, yh, yl, wr, gate, b2, tag)
        w2 = [[sb(f"w2_{n}{i}", [P, FC, D], F32R) for n in ("hi", "lo")] for i in range(2)]
        g = [sb(f"g{i}", [P, BANK]) for i in range(2)]
        gh = [sb(f"g_hi{i}", [P, FC, BANK], F32R) for i in range(2)]
        gl = [sb(f"g_lo{i}", [P, FC, BANK], F32R) for i in range(2)]
        hid = [ctx.enter_context(nc.psum_tensor(f"hid{i}{tag}", [P, BANK], F32)) for i in range(4)]
        out = [ctx.enter_context(nc.psum_tensor(f"eo{i}{tag}", [P, BANK], F32)) for i in range(4)]
        w1_in, w2_in, w_step, w1_ready, w2_ready, b1_in, waits_passed = (
            sem("w1_in"), sem("w2_in"), sem("w_step"), sem("w1_ready"), sem("w2_ready"), [sem("b1_in0"), sem("b1_in1")],
            sem("waits_passed"))
        hid_done, gelu_done, g_hi_done, g_ready = sem("hid_done"), sem("gelu_done"), sem("g_hi_done"), sem("g_ready")
        out_done, added = sem("out_done"), sem("added")
        block = ctx.enter_context(nc.Block())

        def bodies(eng, body):
            body(0, 0)
            with eng.Fori(0, E // 2 - 1) as i:
                body(2 * i + 1, 1)
                body(2 * i + 2, 0)
            body(E - 1, 1)

        @block.sync
        def _(sp):
            def body(e, par):
                after(sp, w1_ready, e)
                sp.dma_start(w1r[:, :, :], w1_d[bass.ds(e, 1), :, :].rearrange("a (c p) n -> p (a c) n", p=P)
                             ).then_inc(w1_in, 16)
                after(sp, gelu_done, 16 * (e - 1))
                sp.dma_start(b1[par][:, :], b1_d[bass.ds(e, 1), :, :].rearrange("a p f -> p (a f)")
                             ).then_inc(b1_in[par], 16)
                after(sp, w2_ready, e)
                sp.dma_start(w2r[:, :, :], w2_d[bass.ds(e, 1), :, :].rearrange("a (f p) n -> p (a f) n", p=P)
                             ).then_inc(w2_in, 16)
            bodies(sp, body)

        @block.gpsimd
        def _(pool):
            def passed(sem_, count):
                pool.wait_ge(sem_, count)
                pool.sem_inc(waits_passed, 1)

            def body(e, par):
                passed(w1_in, 16 * e + 16)
                if not isinstance(e, int) or e >= 2:
                    passed(hid_done, 16 * (e - 1))
                nc.gpsimd.tensor_copy(w1[par][0][:, :, :], w1r[:, :, :]).then_inc(w_step, 1)
                passed(w_step, 2 * e + 1)
                nc.gpsimd.tensor_tensor(w1[par][1][:, :, :], w1r[:, :, :], w1[par][0][:, :, :].bitcast(F32),
                                        ALU.subtract).then_inc(w1_ready, 1)
                passed(w2_in, 16 * e + 16)
                if not isinstance(e, int) or e >= 2:
                    passed(out_done, 8 * (e - 1))
                nc.gpsimd.tensor_copy(w2[par][0][:, :, :], w2r[:, :, :]).then_inc(w_step, 1)
                passed(w_step, 2 * e + 2)
                nc.gpsimd.tensor_tensor(w2[par][1][:, :, :], w2r[:, :, :], w2[par][0][:, :, :].bitcast(F32),
                                        ALU.subtract).then_inc(w2_ready, 1)
            bodies(pool, body)

        @block.tensor
        def _(pe):
            def up(e, par, part):
                pe.wait_ge(w1_ready, e + 1)
                for f in range(FC):
                    u = 16 * e + FC * part + f
                    after(pe, gelu_done, u - 3)
                    for c in range(HALVES):
                        cols, toks = slice(P * f, P * f + P), slice(BANK * part, BANK * part + BANK)
                        ins = split_products(nc, hid[f % 4][:, :], (w1[par][0][:, c, cols], w1[par][1][:, c, cols]),
                                             (yh[:, c, toks], yl[:, c, toks]), c == 0, c == 1)
                    ins.then_inc(hid_done, 1)

            def down(e, par, part):
                pe.wait_ge(w2_ready, e + 1)
                pe.wait_ge(g_ready, 16 * e + FC * part + FC)
                for t in range(4):
                    k = 2 * e + part
                    pe.wait_ge(added, 4 * k + t + 1)
                    for f in range(FC):
                        cols = slice(P * t, P * t + P)
                        ins = split_products(nc, out[t][:, D * part:D * part + D],
                                             (gh[part][:, f, cols], gl[part][:, f, cols]),
                                             (w2[par][0][:, f, :], w2[par][1][:, f, :]), f == 0, f == FC - 1)
                    ins.then_inc(out_done, 1)

            def body(e, par):
                up(e, par, 0)
                if not (isinstance(e, int) and e == 0):
                    down(e - 1, 1 - par, 1)
                up(e, par, 1)
                down(e, par, 0)
            bodies(pe, body)
            down(E - 1, 1, 1)

        @block.scalar
        def _(act):
            def body(e, par):
                act.wait_ge(b1_in[par], 8 * (e - par) + 16)
                for part in range(2):
                    for f in range(FC):
                        u = 16 * e + FC * part + f
                        act.wait_ge(hid_done, u + 1)
                        after(act, g_ready, u - 1)
                        nc.scalar.activation(g[f % 2][:, :], hid[f % 4][:, :], ACT.Gelu,
                                             bias=b1[par][:, f:f + 1]).then_inc(gelu_done, 1)
            bodies(act, body)

        @block.vector
        def _(dve):
            dve.sem_inc(added, 4)

            def add(e, part):
                for t in range(4):
                    k = 2 * e + part
                    tile = chip.x[:, 4 * part + t, :]
                    dve.wait_ge(out_done, 4 * k + t + 1)
                    nc.vector.scalar_tensor_tensor(tile, out[t][:, D * part:D * part + D],
                                                   gate[:, 4 * part + t, bass.ds(e, 1)], tile, ALU.mult,
                                                   ALU.add).then_inc(added, 1)

            def body(e, par):
                for part in range(2):
                    for f in range(FC):
                        u = 16 * e + FC * part + f
                        dve.wait_ge(gelu_done, u + 1)
                        nc.vector.tensor_copy(gh[part][:, f, :], g[f % 2][:, :]).then_inc(g_hi_done, 1)
                        dve.wait_ge(g_hi_done, u + 1)
                        nc.vector.tensor_tensor(gl[part][:, f, :], g[f % 2][:, :], gh[part][:, f, :].bitcast(F32),
                                                ALU.subtract).then_inc(g_ready, 1)
                    if part:
                        add(e, 0)
                    elif not (isinstance(e, int) and e == 0):
                        add(e - 1, 1)
            bodies(dve, body)
            add(E - 1, 1)


def route(nc, chip, yT, yh, yl, wr, gate, b2, tag):
    E = 8
    with ExitStack() as ctx:
        def sb(name, shape, dt=F32):
            return ctx.enter_context(nc.sbuf_tensor(name + tag, shape, dt))

        def sem(name):
            return chip.sem(name + tag)
        logits, key, col = sb("logits", [P, NT, E]), sb("key", [P, NT, E]), [sb(f"col{i}", [P, NT]) for i in range(3)]
        gT = sb("gT", [E, NT, P])
        pl = ctx.enter_context(nc.psum_tensor("pl" + tag, [P, BANK], F32))
        pt = [ctx.enter_context(nc.psum_tensor(f"pt{i}{tag}", [P, BANK], F32)) for i in range(2)]
        pb = [ctx.enter_context(nc.psum_tensor(f"pb{i}{tag}", [P, BANK], F32)) for i in range(4)]
        chain, logits_done, shifted_l, exps, gate_ready, gate_turned, gate_kept, bias_done, hi_done = [
            sem(n) for n in ("rchain", "logits_done", "shifted_l", "exps", "gate_ready", "gate_turned", "gate_kept",
                             "bias_done", "hi_done")]
        block = ctx.enter_context(nc.Block())

        def wide(t):
            return t[:, :].rearrange("p (n o) -> p n o", o=1).to_broadcast([P, NT, E])

        @block.gpsimd
        def _(pool):
            nc.gpsimd.tensor_copy(yh[:, :, :], yT[:, :, :]).then_inc(hi_done, 1)
            pool.wait_ge(hi_done, 1)
            nc.gpsimd.tensor_tensor(yl[:, :, :], yT[:, :, :], yh[:, :, :].bitcast(F32), ALU.subtract)

        @block.tensor
        def _(pe):
            for n in range(NT):
                for c in range(HALVES):
                    ins = nc.tensor.matmul(pl[:, E * n:E * n + E], yT[:, c, P * n:P * n + P], wr[:, c, :],
                                           start=c == 0, stop=c == 1)
            ins.then_inc(logits_done, 1)
            pe.wait_ge(gate_ready, 1)
            for n in range(NT):
                ins = nc.tensor.transpose(pt[n // 4][0:E, P * (n % 4):P * (n % 4) + P], gate[:, n, :], chip.ident)
            ins.then_inc(gate_turned, 1)
            pe.wait_ge(gate_kept, 2)
            for n in range(NT):
                ins = nc.tensor.matmul(pb[n // 2][:, D * (n % 2):D * (n % 2) + D], gT[:, n, :], b2[:, :],
                                       start=True, stop=True)
            ins.then_inc(bias_done, 1)

        @block.scalar
        def _(act):
            act.wait_ge(shifted_l, 1)
            nc.scalar.activation(logits[:, :, :], logits[:, :, :], ACT.Exp).then_inc(exps, 1)

        @block.vector
        def _(dve):
            link = counted(dve, chain)
            dve.wait_ge(logits_done, 1)
            link(nc.vector.tensor_copy(logits[:, :, :], pl[:, 0:NT * E].rearrange("p (n e) -> p n e", e=E)))
            link(nc.vector.tensor_reduce(col[0][:, :], logits[:, :, :], AX.X, ALU.max))
            nc.vector.tensor_tensor(logits[:, :, :], logits[:, :, :], wide(col[0]), ALU.subtract).then_inc(shifted_l, 1)
            dve.wait_ge(exps, 1)
            link(nc.vector.tensor_reduce(col[0][:, :], logits[:, :, :], AX.X, ALU.max))
            link(nc.vector.tensor_reduce(col[1][:, :], logits[:, :, :], AX.X, ALU.add))
            link(nc.vector.reciprocal(col[1][:, :], col[1][:, :]))
            link(nc.vector.tensor_tensor(col[1][:, :], col[0][:, :], col[1][:, :], ALU.mult))
            link(nc.vector.tensor_tensor(key[:, :, :], logits[:, :, :], wide(col[0]), ALU.is_equal))
            link(nc.vector.tensor_tensor(key[:, :, :], key[:, :, :], chip.cst("expert_order").rearrange(
                "p (o e) -> p o e", o=1).to_broadcast([P, NT, E]), ALU.mult))
            link(nc.vector.tensor_reduce(col[2][:, :], key[:, :, :], AX.X, ALU.max))
            link(nc.vector.tensor_tensor(key[:, :, :], key[:, :, :], wide(col[2]), ALU.is_equal))
            nc.vector.tensor_tensor(gate[:, :, :], key[:, :, :], wide(col[1]), ALU.mult).then_inc(gate_ready, 1)
            dve.wait_ge(gate_turned, 1)
            for i in range(2):
                nc.vector.tensor_copy(gT[:, 4 * i:4 * i + 4, :], pt[i][0:E, :].rearrange("p (a c) -> p a c", c=P)
                                      ).then_inc(gate_kept, 1)
            dve.wait_ge(bias_done, 1)
            for i in range(4):
                rows = chip.x[:, 2 * i:2 * i + 2, :]
                nc.vector.tensor_tensor(rows, rows, pb[i][:, :].rearrange("p (a c) -> p a c", c=D), ALU.add)


def differential_stage(nc, chip, dram, tag):
    U, S, KV, HD = 16, T, 8, 8
    LAMBDA_INIT = 0.8 - 0.6 * float(np.exp(-0.3 * 12))
    with ExitStack() as ctx:
        def sb(name, shape, dt=F32):
            return ctx.enter_context(nc.sbuf_tensor(name + tag, shape, dt))

        def sem(name):
            return chip.sem(name + tag)
        yT, wo = sb("yT", [P, HALVES, TOK]), sb("wo", [P, HALVES, D])
        wq, wk, wv = sb("wq", [P, HALVES, 2 * D]), sb("wk", [P, HALVES, D]), sb("wv", [P, HALVES, P])
        lam, gain = sb("lam", [P, 4, HD]), sb("gain", [P, 2 * HD])
        with nc.sbuf_tensor("y" + tag, [P, NT, D], F32) as y:
            def all_rows(a):
                return a.rearrange("(o d) -> o d", o=1).to_broadcast([P, a.shape[0]])
            weights = [(wq[:, :, :], chan(dram["dWq"])), (wk[:, :, :], chan(dram["dWk"])),
                       (wv[:, :, :], chan(dram["L1_attn_Wv"])), (wo[:, :, :], chan(dram["dWo"])),
                       (gain[:, :], all_rows(dram["L1_attn_rms_w"]))]
            weights += [(lam[:, i, :], all_rows(dram["L1_attn_lambda_" + n])) for i, n in
                        enumerate(("q1", "k1", "q2", "k2"))]
            norm_stage(nc, chip, chip.x, y, lambda h, q: yT[:, h, BANK * q:BANK * q + BANK], weights, tag=tag)
        qT, kT, v = sb("qT", [P, 2, TOK]), sb("kT", [P, TOK]), sb("v", [P, NB, P])
        heads = sb("heads", [P, NB, P])
        unit_weight = sb("unit_weight", [P, U])
        with ExitStack() as c2:
            twice = c2.enter_context(nc.sbuf_tensor("twice" + tag, [P, HALVES, NB, 2, T], F32))
            rot = [c2.enter_context(nc.sbuf_tensor(f"rot{i}{tag}", [P, BANK], F32)) for i in range(2)]
            lp, ls = [c2.enter_context(nc.sbuf_tensor(n + tag, s, F32)) for n, s in
                      (("lp", [P, 2, HD]), ("ls", [P, 4]))]
            pj = [c2.enter_context(nc.psum_tensor(f"dj{i}{tag}", [P, BANK], F32)) for i in range(8)]
            chain, projected, rotated, v_done, lam_in, lam_out, doubled = [
                chip.sem(n + tag) for n in ("dchain", "dprojected", "rotated", "dv_done",
                                                                  "lam_in", "lam_out", "doubled")]
            block = c2.enter_context(nc.Block())

            @block.gpsimd
            def _(pool):
                for c in range(HALVES):
                    src = yT[:, c, :].rearrange("p (b t) -> p b t", t=T)
                    for a in range(2):
                        nc.gpsimd.tensor_copy(twice[:, c, :, a, :], src).then_inc(doubled, 1)

            @block.tensor
            def _(pe):
                for i in range(3):
                    for q in range(2):
                        for sw in range(2):
                            bank = (4 * i + 2 * q + sw) % 8
                            if i == 2:
                                pe.wait_ge(rotated, q + 1)
                            w = wq[:, :, D * sw + P * i:D * sw + P * i + P] if i < 2 else wk[:, :, P * sw:P * sw + P]
                            for c in range(HALVES):
                                ins = nc.tensor.matmul(pj[bank][:, :], w[:, c, :], yT[:, c, BANK * q:BANK * q + BANK],
                                                       start=c == 0, stop=c == 1)
                        ins.then_inc(projected, 1)
                pe.wait_ge(doubled, 4)
                for b in range(NB):
                    if b % 4 == 0:
                        pe.wait_ge(rotated, 3 + b // 8)
                    for c in range(HALVES):
                        ins = nc.tensor.matmul(pj[4 + b // 4][:, P * (b % 4):P * (b % 4) + P],
                                               twice[:, c, b, :, :].rearrange("p a t -> p (a t)"),
                                               wv[:, c, :], start=c == 0, stop=c == 1)
                    if b % 4 == 3:
                        ins.then_inc(v_done, 1)

            @block.vector
            def _(dve):
                link = counted(dve, chain)
                for i in range(2):
                    link(nc.vector.tensor_tensor(lp[:, i, :], lam[:, 2 * i, :], lam[:, 2 * i + 1, :], ALU.mult))
                nc.vector.tensor_reduce(ls[:, 0:2], lp[:, :, :], AX.X, ALU.add).then_inc(lam_in, 1)
                for i in range(3):
                    for q in range(2):
                        bank = (4 * i + 2 * q) % 8
                        dve.wait_ge(projected, 2 * i + q + 1)
                        after(dve, rotated, 2 * i + q)
                        for sw, table in enumerate(("cos", "sin")):
                            link(nc.vector.tensor_tensor(
                                rot[sw][:, :].rearrange("p (b t) -> p b t", t=T),
                                pj[bank + sw][:, :].rearrange("p (b t) -> p b t", t=T),
                                chip.cst(table).rearrange("p (o t) -> p o t", o=1).to_broadcast([P, NB // 2, T]),
                                ALU.mult))
                        out = (qT[:, i, :] if i < 2 else kT[:, :])[:, BANK * q:BANK * q + BANK]
                        nc.vector.tensor_tensor(out, rot[0][:, :], rot[1][:, :], ALU.add).then_inc(rotated, 1)
                dve.wait_ge(lam_out, 1)
                link(nc.vector.tensor_tensor(ls[:, 2:3], ls[:, 0:1], ls[:, 1:2], ALU.subtract))
                link(nc.vector.memset(unit_weight[:, :], 1.0))
                link(nc.vector.tensor_scalar(ls[:, 3:4], ls[:, 2:3], LAMBDA_INIT, -1.0, ALU.add, ALU.mult))
                nc.vector.tensor_scalar(unit_weight[:, :].rearrange("p (k m) -> p k m", m=2)[:, :, 1],
                                        unit_weight[:, :].rearrange("p (k m) -> p k m", m=2)[:, :, 1],
                                        ls[:, 3:4], None, ALU.mult)

            @block.scalar
            def _(act):
                act.wait_ge(lam_in, 1)
                nc.scalar.activation(ls[:, 0:2], ls[:, 0:2], ACT.Exp).then_inc(lam_out, 1)
                for i in range(4):
                    act.wait_ge(v_done, i + 1)
                    nc.scalar.activation(v[:, 4 * i:4 * i + 4, :], pj[4 + i][:, :].rearrange("p (a c) -> p a c", c=P),
                                         ACT.Copy)
        causal_maps(nc, chip, qT, kT, v, heads, unit_weight, tag)
        ALL = NB * KV
        with ExitStack() as c3:
            sq = c3.enter_context(nc.sbuf_tensor("sq" + tag, [P, NB, P], F32))
            ms = c3.enter_context(nc.sbuf_tensor("ms" + tag, [P, ALL], F32))
            pt = [c3.enter_context(nc.psum_tensor(f"ht{i}{tag}", [P, BANK], F32)) for i in range(4)]
            chain, squared, mean_ready, root, normed, turned = [
                chip.sem(n + tag) for n in ("nchain", "nsq", "nmean", "nroot", "normed", "nturned")]
            block = c3.enter_context(nc.Block())

            def groups(t):
                return t[:, :, :].rearrange("p b (k d) -> p (b k) d", d=2 * HD)

            @block.scalar
            def _(act):
                nc.scalar.activation(sq[:, :, :], heads[:, :, :], ACT.Square).then_inc(squared, 1)
                act.wait_ge(mean_ready, 1)
                nc.scalar.activation(ms[:, :], ms[:, :], ACT.Sqrt).then_inc(root, 1)
                for i in range(4):
                    act.wait_ge(turned, i + 1)
                    nc.scalar.activation(
                        qT[:, :, 4 * T * i:4 * T * i + 4 * T].rearrange("p r (b t) -> p b r t", t=T),
                        pt[i][:, :].rearrange("p (b r t) -> p b r t", r=2, t=T), ACT.Copy)

            @block.vector
            def _(dve):
                link = counted(dve, chain)
                link(nc.vector.tensor_scalar(gain[:, :], gain[:, :], 1.0 - LAMBDA_INIT, None, ALU.mult))
                dve.wait_ge(squared, 1)
                link(nc.vector.tensor_reduce(ms[:, :], groups(sq), AX.X, ALU.add))
                nc.vector.tensor_scalar(ms[:, :], ms[:, :], 1.0 / (2 * HD), 1e-6, ALU.mult,
                                        ALU.add).then_inc(mean_ready, 1)
                dve.wait_ge(root, 1)
                link(nc.vector.reciprocal(ms[:, :], ms[:, :]))
                link(nc.vector.tensor_tensor(groups(heads), groups(heads), ms[:, :].rearrange(
                    "p (a o) -> p a o", o=1).to_broadcast([P, ALL, 2 * HD]), ALU.mult))
                nc.vector.tensor_tensor(groups(heads), groups(heads), gain[:, :].rearrange(
                    "p (o d) -> p o d", o=1).to_broadcast([P, ALL, 2 * HD]), ALU.mult).then_inc(normed, 1)

            @block.tensor
            def _(pe):
                pe.wait_ge(normed, 1)
                for b in range(NB):
                    ins = nc.tensor.transpose(pt[b // 4][:, P * (b % 4):P * (b % 4) + P], heads[:, b, :], chip.ident)
                    if b % 4 == 3:
                        ins.then_inc(turned, 1)
        output_stage(nc, chip, qT, wo, None, tag)


def causal_maps(nc, chip, qT, kT, v, heads, unit_weight, tag):
    U, KV, HD = 16, 8, 8
    with ExitStack() as ctx:
        def sb(name, shape, dt=F32):
            return ctx.enter_context(nc.sbuf_tensor(name + tag, shape, dt))

        def sem(name):
            return chip.sem(name + tag)
        kb = [sb(f"k_block{i}", [P, U, T]) for i in range(2)]
        qs, vs = [[sb(f"{n}_now{i}", [P, P]) for i in range(2)] for n in ("q", "v")]
        sc = [sb(f"sc{i}", [P, U, T]) for i in range(2)]
        mx, sm, rc = [sb(n, [P, 2, U]) for n in ("umax", "usum", "urec")]
        diff = [sb(f"diff{i}", [P, KV, T]) for i in range(2)]
        dT = [sb(f"dT{i}", [P, 4, P]) for i in range(2)]
        ps = [ctx.enter_context(nc.psum_tensor(f"ds{i}{tag}", [P, 2 * BANK], F32)) for i in range(2)]
        pt = [ctx.enter_context(nc.psum_tensor(f"dt{i}{tag}", [P, BANK], F32)) for i in range(2)]
        po = [ctx.enter_context(nc.psum_tensor(f"do{i}{tag}", [P, BANK], F32)) for i in range(2)]
        blocks_ready, scored, shifted, exp_done, waits_passed = (sem("blocks_ready"), sem("scored"), sem("shifted"),
                                                                 sem("exp_done"), sem("waits_passed"))
        taken, maxed, weight_step, diffed, turned, moved, valued, kept = [
            sem("m_" + n) for n in ("taken", "maxed", "weight_step", "diffed", "turned", "moved", "valued", "kept")]
        block = ctx.enter_context(nc.Block())

        def wide(a):
            return a.rearrange("p (u o) -> p u o", o=1).to_broadcast([P, U, T])

        def bodies(eng, body):
            body(0, 0)
            body(1, 1)
            with eng.Fori(1, NB // 2) as i:
                body(2 * i, 0)
                body(2 * i + 1, 1)

        def known(b, least):
            return not isinstance(b, int) or b >= least

        @block.gpsimd
        def _(pool):
            def passed(sem_, count):
                pool.wait_ge(sem_, count)
                pool.sem_inc(waits_passed, 1)

            def body(b, par):
                if known(b, 2):
                    passed(scored, b - 1)
                nc.gpsimd.tensor_tensor(kb[par][:, :, :],
                                        kT[:, bass.ds(T * b, T)].rearrange("p (o t) -> p o t", o=1)
                                        .to_broadcast([P, U, T]), wide(chip.cst("unit_rows")), ALU.mult)
                nc.gpsimd.tensor_copy(qs[par][:, :].rearrange("p (r t) -> p r t", t=T), qT[:, :, bass.ds(T * b, T)])
                if known(b, 2):
                    passed(valued, b - 1)
                nc.gpsimd.tensor_tensor(vs[par][:, :], v[:, bass.ds(b, 1), :].rearrange("p o c -> p (o c)"),
                                        chip.cst("row_half_of_head"), ALU.mult).then_inc(blocks_ready, 1)
                passed(maxed, b + 1)
                nc.gpsimd.tensor_tensor(sc[par][:, :, :], sc[par][:, :, :], wide(mx[:, par, :]),
                                        ALU.subtract).then_inc(shifted, 1)
            bodies(pool, body)

        @block.tensor
        def _(pe):
            def scores(b, par):
                pe.wait_ge(blocks_ready, b + 1)
                after(pe, taken, b - 1)
                for i in range(2):
                    ins = nc.tensor.matmul(ps[par][:, BANK * i:BANK * i + BANK], qs[par][:, :],
                                           kb[par][:, 8 * i:8 * i + 8, :].rearrange("p u t -> p (u t)"),
                                           start=True, stop=True)
                ins.then_inc(scored, 1)

            def values(b, par):
                pe.wait_ge(diffed, b + 1)
                for c in range(4):
                    ins = nc.tensor.transpose(pt[par][:, P * c:P * c + P],
                                              diff[par][:, 2 * c:2 * c + 2, :].rearrange("p k t -> p (k t)"),
                                              chip.ident)
                ins.then_inc(turned, 1)
                pe.wait_ge(moved, b + 1)
                after(pe, kept, b - 1)
                for c in range(4):
                    ins = nc.tensor.matmul(po[par][:, 4 * HD * c:4 * HD * c + 4 * HD], dT[par][:, c, :],
                                           vs[par][:, 4 * HD * c:4 * HD * c + 4 * HD], start=True, stop=True)
                ins.then_inc(valued, 1)

            def body(b, par):
                scores(b, par)
                if known(b, 1):
                    values(b - 1, 1 - par)
            bodies(pe, body)
            values(NB - 1, 1)

        @block.scalar
        def _(act):
            def move(b, par):
                act.wait_ge(turned, b + 1)
                nc.scalar.activation(dT[par][:, :, :], pt[par][:, :].rearrange("p (a c) -> p a c", c=P),
                                     ACT.Copy).then_inc(moved, 1)

            def body(b, par):
                act.wait_ge(shifted, b + 1)
                nc.scalar.activation(sc[par][:, :, :], sc[par][:, :, :], ACT.Exp).then_inc(exp_done, 1)
                if known(b, 1):
                    move(b - 1, 1 - par)
            bodies(act, body)
            move(NB - 1, 1)

        @block.vector
        def _(dve):
            def take(b, par):
                dve.wait_ge(scored, b + 1)
                nc.vector.scalar_tensor_tensor(
                    sc[par][:, :, :], ps[par][:, :].rearrange("p (u t) -> p u t", t=T), HD ** -0.5,
                    chip.cst("causal").rearrange("p (o t) -> p o t", o=1).to_broadcast([P, U, T]),
                    ALU.mult, ALU.add).then_inc(taken, 1)
                dve.wait_ge(taken, b + 1)
                nc.vector.tensor_reduce(mx[:, par, :], sc[par][:, :, :], AX.X, ALU.max).then_inc(maxed, 1)

            def weigh(b, par):
                def step(ins, k):
                    ins.then_inc(weight_step, 1)
                    dve.wait_ge(weight_step, 4 * b + k)
                dve.wait_ge(exp_done, b + 1)
                step(nc.vector.tensor_reduce(sm[:, par, :], sc[par][:, :, :], AX.X, ALU.add), 1)
                step(nc.vector.reciprocal(rc[:, par, :], sm[:, par, :]), 2)
                step(nc.vector.tensor_tensor(rc[:, par, :], rc[:, par, :], unit_weight[:, :], ALU.mult), 3)
                step(nc.vector.tensor_tensor(sc[par][:, :, :], sc[par][:, :, :], wide(rc[:, par, :]), ALU.mult), 4)
                maps = sc[par][:, :, :].rearrange("p (k m) t -> p k m t", m=2)
                nc.vector.tensor_tensor(diff[par][:, :, :], maps[:, :, 0, :], maps[:, :, 1, :],
                                        ALU.add).then_inc(diffed, 1)

            def keep(b, par):
                dve.wait_ge(valued, b + 1)
                nc.vector.tensor_scalar(heads[:, bass.ds(b, 1), :].rearrange("p o c -> p (o c)"), po[par][:, 0:P],
                                        1.0, None, ALU.mult).then_inc(kept, 1)

            def body(b, par):
                take(b, par)
                if known(b, 2):
                    keep(b - 2, par)
                if known(b, 1):
                    weigh(b - 1, 1 - par)
            bodies(dve, body)
            keep(NB - 2, 0)
            weigh(NB - 1, 1)
            keep(NB - 1, 1)


def depths_stage(nc, chip, dram, tag):
    KEPT = float(int(T * 0.75))
    with ExitStack() as ctx:
        def sb(name, shape, dt=F32):
            return ctx.enter_context(nc.sbuf_tensor(name + tag, shape, dt))

        def sem(name):
            return chip.sem(name + tag)
        y, yT, w, wr = sb("y", [P, NT, D]), sb("yT", [P, HALVES, TOK]), sb("w", [P, HALVES, D]), sb("wr", [P, D])
        norm_stage(nc, chip, chip.x, y, lambda h, q: yT[:, h, BANK * q:BANK * q + BANK],
                   [(w[:, :, :], chan(dram["L1_ffn_w_block"])),
                    (wr[:, :], dram["L1_ffn_w_router"].rearrange("(o d) -> o d", o=1).to_broadcast([P, D]))], tag=tag)
        prod, out = sb("prod", [P, NT, D]), sb("gelu", [P, NT, D])
        score, mine, rank, rest = [sb(n, [P, NT]) for n in ("score", "mine", "rank", "rest")]
        own, others, above, equal = [sb(n, [P, NT, T]) for n in ("own", "others", "above", "equal")]
        pr = ctx.enter_context(nc.psum_tensor("pr" + tag, [P, BANK], F32))
        pm = [ctx.enter_context(nc.psum_tensor(f"pm{i}{tag}", [P, BANK], F32)) for i in range(4)]
        chain, own_ready, spread, projected, gelus = [sem(n) for n in ("fchain", "own_ready", "spread", "fprojected",
                                                                       "gelus")]
        block = ctx.enter_context(nc.Block())

        def wide(t, n):
            return t[:, :].rearrange("p (n o) -> p n o", o=1).to_broadcast([P, NT, n])

        def table(name):
            return chip.cst(name).rearrange("p (o t) -> p o t", o=1).to_broadcast([P, NT, T])

        @block.tensor
        def _(pe):
            for n in range(NT):
                for c in range(HALVES):
                    ins = nc.tensor.matmul(pm[n // 2][:, D * (n % 2):D * (n % 2) + D], yT[:, c, P * n:P * n + P],
                                           w[:, c, :], start=c == 0, stop=c == 1)
                if n % 2:
                    ins.then_inc(projected, 1)
            pe.wait_ge(own_ready, 1)
            nc.tensor.matmul(pr[:, :], chip.cst("same_sequence"), own[:, :, :].rearrange("p n t -> p (n t)"),
                             start=True, stop=True).then_inc(spread, 1)

        @block.scalar
        def _(act):
            for i in range(4):
                act.wait_ge(projected, i + 1)
                nc.scalar.activation(out[:, 2 * i:2 * i + 2, :], pm[i][:, :].rearrange("p (a c) -> p a c", c=D),
                                     ACT.Gelu_apprx_tanh).then_inc(gelus, 1)

        @block.vector
        def _(dve):
            link = counted(dve, chain)
            link(nc.vector.tensor_tensor(prod[:, :, :], y[:, :, :], wr[:, :].rearrange("p (o d) -> p o d", o=1)
                                         .to_broadcast([P, NT, D]), ALU.mult))
            link(nc.vector.tensor_reduce(score[:, :], prod[:, :, :], AX.X, ALU.add))
            nc.vector.tensor_tensor(own[:, :, :], table("own_column"), wide(score, T), ALU.mult).then_inc(own_ready, 1)
            dve.wait_ge(spread, 1)
            link(nc.vector.tensor_copy(others[:, :, :], pr[:, :].rearrange("p (n t) -> p n t", t=T)))
            link(nc.vector.tensor_tensor(own[:, :, :], table("own_column"), others[:, :, :], ALU.mult))
            link(nc.vector.tensor_reduce(mine[:, :], own[:, :, :], AX.X, ALU.add))
            link(nc.vector.tensor_tensor(above[:, :, :], others[:, :, :], wide(mine, T), ALU.is_gt))
            link(nc.vector.tensor_tensor(equal[:, :, :], others[:, :, :], wide(mine, T), ALU.is_equal))
            link(nc.vector.tensor_tensor(equal[:, :, :], equal[:, :, :], table("earlier_column"), ALU.mult))
            link(nc.vector.tensor_tensor(above[:, :, :], above[:, :, :], equal[:, :, :], ALU.add))
            link(nc.vector.tensor_reduce(rank[:, :], above[:, :, :], AX.X, ALU.add))
            link(nc.vector.tensor_scalar(rest[:, :], rank[:, :], KEPT, None, ALU.is_ge))
            link(nc.vector.tensor_scalar(rank[:, :], rank[:, :], KEPT, None, ALU.is_lt))
            for n in range(NT):
                link(nc.vector.scalar_tensor_tensor(chip.x[:, n, :], y[:, n, :], rest[:, n:n + 1], chip.x[:, n, :],
                                                    ALU.mult, ALU.add))
            for n in range(NT):
                dve.wait_ge(gelus, n // 2 + 1)
                nc.vector.scalar_tensor_tensor(chip.x[:, n, :], out[:, n, :], rank[:, n:n + 1], chip.x[:, n, :],
                                               ALU.mult, ALU.add)


def cross_stage(nc, chip, dram, layer, tag, mask):
    with ExitStack() as ctx:
        def sb(name, shape, dt=F32):
            return ctx.enter_context(nc.sbuf_tensor(name + tag, shape, dt))
        qT, wo = sb("qT", [P, HALVES, TOK]), sb("wo", [P, HALVES, D])
        bq, bk, bv, bo = sb("bq", [P, HALVES]), sb("bk", [P, HALVES]), sb("bv", [P, HALVES]), sb("bo", [1, D])
        with ExitStack() as ctx2:
            split = [[ctx2.enter_context(nc.sbuf_tensor(n + tag, [P, HALVES, D], F32R))
                      for n in (w + "_hi", w + "_lo")] for w in ("wk", "wv")]
            with ExitStack() as ctx3:
                y, yT, wq, wk, wv = [ctx3.enter_context(nc.sbuf_tensor(n + tag, [P, *s], F32)) for n, s in
                                     (("y", [NT, D]), ("yT", [HALVES, TOK]), ("wq", [HALVES, D]),
                                      ("wk", [HALVES, D]), ("wv", [HALVES, D]))]
                weights = [(t[:, :, :], chan(dram[layer + n])) for t, n in
                           ((wq, "Wq"), (wk, "Wk"), (wv, "Wv"), (wo, "Wo"))]
                if mask is not None:
                    weights += [(t[:, :], dram[layer + n]) for t, n in
                                ((bq, "bq"), (bk, "bk"), (bv, "bv"))]
                    weights.append((bo[:, :], dram[layer + "bo"].rearrange("(a c) -> a c", a=1)))
                else:
                    zero_tiles(nc, [bq, bk, bv], tag)
                norm_stage(nc, chip, chip.x, y, lambda h, q: yT[:, h, BANK * q:BANK * q + BANK], weights, tag=tag)
                query_stage(nc, chip, yT, wq, bq, 1.0 if mask is None else 0.25, qT, wk, wv, split, tag)
            cross_attention(nc, chip, dram["ctxT"], qT, qT, *split, bk, bv, mask, tag)
        output_stage(nc, chip, qT, wo, None if mask is None else bo[:, :], tag)


def zero_tiles(nc, tiles, tag):
    with ExitStack() as ctx:
        block = ctx.enter_context(nc.Block())

        @block.vector
        def _(dve):
            for t in tiles:
                nc.vector.memset(t[:, :], 0.0)


def store(nc, chip, out):
    with ExitStack() as ctx:
        stored = chip.sem("stored")
        block = ctx.enter_context(nc.Block())

        @block.sync
        def _(sp):
            sp.dma_start(out.rearrange("n p c -> p n c"), chip.x[:, :, :]).then_inc(stored, 16)
            sp.wait_ge(stored, 16)


STAGES = "ABCDEF"


def build(nc, dram, out):
    with ExitStack() as ctx:
        chip = Chip(nc)
        chip.x = ctx.enter_context(nc.sbuf_tensor("x", [P, NT, D], F32))
        chip.const = ctx.enter_context(nc.sbuf_tensor("const", list(CONSTANTS.shape), F32))
        chip.cst = lambda name: chip.const[:, CONST[name][0]:CONST[name][0] + CONST[name][1]]
        chip.ident = chip.cst("ident")
        load_constants(nc, chip, dram)
        if "A" in STAGES:
            cross_stage(nc, chip, dram, "L0_xattn_", "_a", None)
            chip.end_stage()
        if "B" in STAGES:
            rwkv_stage(nc, chip, dram, "_b")
            chip.end_stage()
        if "C" in STAGES:
            experts_stage(nc, chip, dram, "_c")
            chip.end_stage()
        if "D" in STAGES:
            cross_stage(nc, chip, dram, "L1_xattn_", "_d", dram["mask"])
            chip.end_stage()
        if "E" in STAGES:
            differential_stage(nc, chip, dram, "_e")
            chip.end_stage()
        if "F" in STAGES:
            depths_stage(nc, chip, dram, "_f")
        store(nc, chip, out)


COLUMNS = ["L0_attn_" + n for n in ("ln1_g", "ln1_b", "ln2_g", "ln2_b", "time_first", "mix_k", "mix_v", "mix_r",
                                     "cmix_k", "cmix_r")] + ["L1_xattn_" + n for n in ("bq", "bk", "bv")]


def laid_out(inputs):
    a = {k: np.asarray(v) for k, v in inputs.items()}
    o = {"x": a["x"].reshape(NT, P, D), "constants": CONSTANTS, "ctxT": a["ctx_1024"].transpose(0, 2, 1),
         "mask": a["mask_Bx1xSxS2_fk0"].reshape(NB, T, KEYS)}
    for k, v in a.items():
        if k.startswith(("L0_", "L1_")):
            o[k] = v
    for k in ("Wk_t", "Wv_t", "Wr_t", "Wk_c", "Wv_c", "Wr_c"):
        o["L0_attn_" + k] = a["L0_attn_" + k].T
    for k in ("Wq", "Wk", "Wv", "Wo"):
        o["L1_xattn_" + k] = a["L1_xattn_" + k].T
    for n in COLUMNS:
        o[n] = a[n].reshape(HALVES, P).T
    o["L0_ffn_b1"] = a["L0_ffn_b1"].reshape(8, 8, P).transpose(0, 2, 1)
    wq = a["L1_attn_Wq"].reshape(D, 8, 2, 2, 8).transpose(0, 2, 1, 3, 4)
    wk = a["L1_attn_Wk"].reshape(D, 8, 2, 8)
    swap = [4, 5, 6, 7, 0, 1, 2, 3]
    o["dWq"] = np.concatenate([wq.reshape(D, D), wq[..., swap].reshape(D, D)], axis=1)
    o["dWk"] = np.concatenate([wk.reshape(D, P), wk[..., swap].reshape(D, P)], axis=1)
    o["dWo"] = a["L1_attn_Wo"].reshape(8, 2, 16, D).transpose(1, 0, 2, 3).reshape(D, D)
    return {k: np.ascontiguousarray(v) for k, v in o.items()}


def kernel(**inputs):
    import concourse.bacc as bacc
    from concourse.bass_utils import run_bass_kernel_spmd

    nc = bacc.Bacc("TRN2", target_bir_lowering=False, num_devices=1)
    arrays = laid_out(inputs)
    dram = {k: nc.dram_tensor("in_" + k, v.shape, mybir.dt.from_np(v.dtype), kind="ExternalInput").ap()
            for k, v in arrays.items()}
    out = nc.dram_tensor("out", (NT, P, D), F32, kind="ExternalOutput").ap()
    build(nc, dram, out)
    return run_bass_kernel_spmd(nc, [{"in_" + k: v for k, v in arrays.items()}], core_ids=[0]).results[0]["out"].reshape(NB, T, D)
```
